# Optimizing a Trainium2 kernel written in Bass

```python
import numpy as np
import jax
import jax.numpy as jnp

def _softmax(x, axis=-1):
    return jax.nn.softmax(x, axis=axis)

def _gelu(x):
    return jax.nn.gelu(x, approximate=True)

def _silu(x):
    return jax.nn.silu(x)

def _sigmoid(x):
    return jax.nn.sigmoid(x)

def _layernorm(x, axis=-1, eps=1e-05):
    m = jnp.mean(x, axis=axis, keepdims=True)
    v = jnp.var(x, axis=axis, keepdims=True)
    return (x - m) / jnp.sqrt(v + eps)

def _scatter_add(tgt, idx, src, axis=0):
    return tgt.at[idx].add(src)

def _segment_sum(src, seg, n):
    return jax.ops.segment_sum(src, seg, n)
kernel_name = 'mk_seq_postln_d2_jaxref_r8_558f04'

def setup_inputs(seed: int=0):
    np.random.seed(seed)
    _w = jnp.asarray

    def _L0_attn_setup():
        import jax, jax.numpy as jnp
        import numpy as np
        B, S, HID = (2, 128, 512)
        N_HEADS, N_KV_HEADS = (32, 8)
        HEAD_DIM = HID // N_HEADS
        N_REP = N_HEADS // N_KV_HEADS
        ROPE_THETA = 10000.0

        def _rope(x, cos, sin):
            xe = x[..., 0::2]
            xo = x[..., 1::2]
            oe = xe * cos - xo * sin
            oo = xe * sin + xo * cos
            return jnp.stack([oe, oo], axis=-1).reshape(x.shape)
        key = jax.random.key(seed)
        ks = jax.random.split(key, 5)
        scale = 0.02
        return {'hidden_states': jax.random.normal(ks[0], (B, S, HID), dtype=jnp.float32), 'Wq': jax.random.normal(ks[1], (HID, HID), dtype=jnp.float32) * scale, 'Wk': jax.random.normal(ks[2], (N_KV_HEADS * HEAD_DIM, HID), dtype=jnp.float32) * scale, 'Wv': jax.random.normal(ks[3], (N_KV_HEADS * HEAD_DIM, HID), dtype=jnp.float32) * scale, 'Wo': jax.random.normal(ks[4], (HID, HID), dtype=jnp.float32) * scale}
    _L0_attn_in = _L0_attn_setup()

    def _L0_ffn_setup():
        import jax, jax.numpy as jnp
        import numpy as np
        HIDDEN = 512
        INTER = 1376
        GROUPSIZE = 128
        PACK = 8

        def dequant_gptq(qweight, scales, zeros, groupsize):
            K = qweight.shape[0] * PACK
            N = qweight.shape[1]
            k = jnp.arange(K)
            q = qweight[k // PACK, :] >> (k % PACK * 4)[:, None] & 15
            n = jnp.arange(N)
            z = zeros[:, n // PACK] >> (n % PACK * 4)[None, :] & 15
            s = scales.astype(jnp.float32)
            zp = (z.astype(jnp.float32) + 1.0) * s
            g = k // groupsize
            return q.astype(jnp.float32) * s[g] - zp[g]
        key = jax.random.key(seed)
        ks = jax.random.split(key, 11)
        imax = 2147483647
        G_h = HIDDEN // GROUPSIZE
        G_i = (INTER + GROUPSIZE - 1) // GROUPSIZE
        x = (jax.random.normal(ks[0], (2, 256, HIDDEN), dtype=jnp.float32) * 0.5).astype(jnp.float16)
        return {'x': x, 'gate_qweight': jax.random.randint(ks[1], (HIDDEN // PACK, INTER), 0, imax, dtype=jnp.int32), 'gate_scales': (jax.random.uniform(ks[2], (G_h, INTER), dtype=jnp.float32) * 0.01 + 0.001).astype(jnp.float16), 'gate_zeros': jax.random.randint(ks[3], (G_h, INTER // PACK), 0, imax, dtype=jnp.int32), 'up_qweight': jax.random.randint(ks[4], (HIDDEN // PACK, INTER), 0, imax, dtype=jnp.int32), 'up_scales': (jax.random.uniform(ks[5], (G_h, INTER), dtype=jnp.float32) * 0.01 + 0.001).astype(jnp.float16), 'up_zeros': jax.random.randint(ks[6], (G_h, INTER // PACK), 0, imax, dtype=jnp.int32), 'down_qweight': jax.random.randint(ks[7], (INTER // PACK, HIDDEN), 0, imax, dtype=jnp.int32), 'down_scales': (jax.random.uniform(ks[8], (G_i, HIDDEN), dtype=jnp.float32) * 0.01 + 0.001).astype(jnp.float16), 'down_zeros': jax.random.randint(ks[9], (G_i, HIDDEN // PACK), 0, imax, dtype=jnp.int32)}
    _L0_ffn_in = _L0_ffn_setup()

    def _L1_attn_setup():
        import jax, jax.numpy as jnp
        import numpy as np
        HID = 512
        DM = 128
        DIN = 2 * DM
        DST = 16
        HD = 64
        NH = DIN // HD
        DCONV = 7
        CONV_DIM = DIN + 2 * DST
        DIN_PROJ = 2 * DIN + 2 * DST + 2 * NH
        SEQ, BATCH = (256, 4)

        def _causal_conv(x, w, b):
            y = jax.lax.conv_general_dilated(jnp.transpose(x, (0, 2, 1)), w, (1,), [(DCONV - 1, 0)], feature_group_count=CONV_DIM, dimension_numbers=('NCH', 'OIH', 'NCH'))
            return jnp.transpose(y, (0, 2, 1)) + b

        def _ssm_scan(x, dt, A, B, C):
            dA = jnp.exp(dt * A)
            dBx = dt[..., None] * x

            def step(h, t):
                dA_t, dBx_t, B_t, C_t = t
                h = dA_t[:, :, None, None] * h + dBx_t[..., None] * B_t[:, None, None, :]
                y = jnp.einsum('bhpn,bn->bhp', h, C_t)
                return (h, y)
            h0 = jnp.zeros((x.shape[0], NH, HD, DST), x.dtype)
            _, ys = jax.lax.scan(step, h0, (jnp.moveaxis(dA, 1, 0), jnp.moveaxis(dBx, 1, 0), jnp.moveaxis(B, 1, 0), jnp.moveaxis(C, 1, 0)))
            return jnp.moveaxis(ys, 0, 1)

        def _hydra(u, in_w, conv_w, conv_b, dt_bias, A_log, D, fcD_w, norm_w, out_w):
            b, l, _ = u.shape
            zxbcdt = u @ in_w.T
            z = zxbcdt[..., :DIN]
            xBC = zxbcdt[..., DIN:DIN + CONV_DIM]
            dt2 = zxbcdt[..., DIN + CONV_DIM:]
            dt_fw = jax.nn.softplus(dt2[..., :NH] + dt_bias)
            dt_bw = jax.nn.softplus(jnp.flip(dt2[..., NH:], 1) + dt_bias)
            xBC = jax.nn.silu(_causal_conv(xBC, conv_w, conv_b))
            xs = xBC[..., :DIN]
            Bm = xBC[..., DIN:DIN + DST]
            Cm = xBC[..., DIN + DST:]
            A = -jnp.exp(A_log)
            x4 = xs.reshape(b, l, NH, HD)
            y_fw = _ssm_scan(x4, dt_fw, A, Bm, Cm).reshape(b, l, DIN)
            y_bw = jnp.flip(_ssm_scan(jnp.flip(x4, 1), dt_bw, A, jnp.flip(Bm, 1), jnp.flip(Cm, 1)).reshape(b, l, DIN), 1)
            zero = jnp.zeros((b, 1, DIN), u.dtype)
            y = jnp.concatenate([zero, y_fw[:, :-1]], 1) + jnp.concatenate([y_bw[:, 1:], zero], 1)
            y = y + xs * jnp.repeat(xs @ fcD_w.T + D, HD, axis=-1)
            yz = y * jax.nn.silu(z)
            y = yz * jax.lax.rsqrt(jnp.mean(jnp.square(yz), -1, keepdims=True) + 1e-05) * norm_w
            return y @ out_w.T
        key = jax.random.key(seed)
        ks = jax.random.split(key, 12)
        rn = lambda k, shape, s=0.02: jax.random.normal(k, shape, jnp.float32) * s
        dt = jnp.exp(jax.random.uniform(ks[5], (NH,), jnp.float32, np.log(0.001), np.log(0.1)))
        return dict(x=jax.random.normal(ks[0], (SEQ, BATCH, HID), jnp.float32), w_down=rn(ks[1], (DM, HID)), b_down=jnp.zeros((DM,), jnp.float32), w_up=rn(ks[2], (HID, DM)), b_up=jnp.zeros((HID,), jnp.float32), gate1=jnp.asarray(0.6, jnp.float32), hy_in_w=rn(ks[3], (DIN_PROJ, DM)), hy_conv_w=rn(ks[4], (CONV_DIM, 1, DCONV), 0.2), hy_conv_b=jnp.zeros((CONV_DIM,), jnp.float32), hy_dt_bias=jnp.log(jnp.expm1(dt)), hy_A_log=jnp.log(jax.random.uniform(ks[6], (NH,), jnp.float32, 1.0, 16.0)), hy_D=jnp.ones((NH,), jnp.float32), hy_fcD_w=rn(ks[7], (NH, DIN)), hy_norm_w=jnp.ones((DIN,), jnp.float32), hy_out_w=rn(ks[8], (DM, DIN)))
    _L1_attn_in = _L1_attn_setup()

    def _L1_ffn_setup():
        import jax, jax.numpy as jnp
        import numpy as np
        GROUP_SIZE = 128

        def dequantize(imatrix, scales, zeros, group_size, out_dtype):
            rs = jnp.repeat(scales, group_size, axis=0)
            rz = jnp.repeat(zeros, group_size, axis=0)
            return ((imatrix.astype(rs.dtype) - rz.astype(rs.dtype)) * rs).astype(out_dtype)
        key = jax.random.key(seed)
        ks = jax.random.split(key, 10)
        H, I, G = (512, 1792, GROUP_SIZE)
        B, S = (4, 256)
        x = jax.random.normal(ks[0], (B, S, H), dtype=jnp.float32)
        gate_w = jax.random.randint(ks[1], (H, I), 0, 16, dtype=jnp.int32)
        gate_z = jax.random.randint(ks[2], (H // G, I), 0, 16, dtype=jnp.int32)
        gate_s = jax.random.uniform(ks[3], (H // G, I), dtype=jnp.float32) * 0.01
        up_w = jax.random.randint(ks[4], (H, I), 0, 16, dtype=jnp.int32)
        up_z = jax.random.randint(ks[5], (H // G, I), 0, 16, dtype=jnp.int32)
        up_s = jax.random.uniform(ks[6], (H // G, I), dtype=jnp.float32) * 0.01
        down_w = jax.random.randint(ks[7], (I, H), 0, 16, dtype=jnp.int32)
        down_z = jax.random.randint(ks[8], (I // G, H), 0, 16, dtype=jnp.int32)
        down_s = jax.random.uniform(ks[9], (I // G, H), dtype=jnp.float32) * 0.01
        return {'x': x, 'gate_w': gate_w, 'gate_z': gate_z, 'gate_s': gate_s, 'up_w': up_w, 'up_z': up_z, 'up_s': up_s, 'down_w': down_w, 'down_z': down_z, 'down_s': down_s}
    _L1_ffn_in = _L1_ffn_setup()
    _d = {'L0_attn_hidden_states': _L0_attn_in['hidden_states'], 'L0_attn_Wq': _L0_attn_in['Wq'], 'L0_attn_Wk': _L0_attn_in['Wk'], 'L0_attn_Wv': _L0_attn_in['Wv'], 'L0_attn_Wo': _L0_attn_in['Wo'], 'L0_ffn_gate_qweight': _L0_ffn_in['gate_qweight'], 'L0_ffn_gate_scales': _L0_ffn_in['gate_scales'], 'L0_ffn_gate_zeros': _L0_ffn_in['gate_zeros'], 'L0_ffn_up_qweight': _L0_ffn_in['up_qweight'], 'L0_ffn_up_scales': _L0_ffn_in['up_scales'], 'L0_ffn_up_zeros': _L0_ffn_in['up_zeros'], 'L0_ffn_down_qweight': _L0_ffn_in['down_qweight'], 'L0_ffn_down_scales': _L0_ffn_in['down_scales'], 'L0_ffn_down_zeros': _L0_ffn_in['down_zeros'], 'L1_attn_w_down': _L1_attn_in['w_down'], 'L1_attn_b_down': _L1_attn_in['b_down'], 'L1_attn_w_up': _L1_attn_in['w_up'], 'L1_attn_b_up': _L1_attn_in['b_up'], 'L1_attn_gate1': _L1_attn_in['gate1'], 'L1_attn_hy_in_w': _L1_attn_in['hy_in_w'], 'L1_attn_hy_conv_w': _L1_attn_in['hy_conv_w'], 'L1_attn_hy_conv_b': _L1_attn_in['hy_conv_b'], 'L1_attn_hy_dt_bias': _L1_attn_in['hy_dt_bias'], 'L1_attn_hy_A_log': _L1_attn_in['hy_A_log'], 'L1_attn_hy_D': _L1_attn_in['hy_D'], 'L1_attn_hy_fcD_w': _L1_attn_in['hy_fcD_w'], 'L1_attn_hy_norm_w': _L1_attn_in['hy_norm_w'], 'L1_attn_hy_out_w': _L1_attn_in['hy_out_w'], 'L1_ffn_gate_w': _L1_ffn_in['gate_w'], 'L1_ffn_gate_z': _L1_ffn_in['gate_z'], 'L1_ffn_gate_s': _L1_ffn_in['gate_s'], 'L1_ffn_up_w': _L1_ffn_in['up_w'], 'L1_ffn_up_z': _L1_ffn_in['up_z'], 'L1_ffn_up_s': _L1_ffn_in['up_s'], 'L1_ffn_down_w': _L1_ffn_in['down_w'], 'L1_ffn_down_z': _L1_ffn_in['down_z'], 'L1_ffn_down_s': _L1_ffn_in['down_s']}
    _x0 = _d['L0_attn_hidden_states']
    _d['L0_attn_hidden_states'] = jax.random.normal(jax.random.fold_in(jax.random.key(seed), 1), (4, 512, 512), dtype=_x0.dtype)
    del _x0
    return _d

def reference(L0_attn_hidden_states, L0_attn_Wq, L0_attn_Wk, L0_attn_Wv, L0_attn_Wo, L0_ffn_gate_qweight, L0_ffn_gate_scales, L0_ffn_gate_zeros, L0_ffn_up_qweight, L0_ffn_up_scales, L0_ffn_up_zeros, L0_ffn_down_qweight, L0_ffn_down_scales, L0_ffn_down_zeros, L1_attn_w_down, L1_attn_b_down, L1_attn_w_up, L1_attn_b_up, L1_attn_gate1, L1_attn_hy_in_w, L1_attn_hy_conv_w, L1_attn_hy_conv_b, L1_attn_hy_dt_bias, L1_attn_hy_A_log, L1_attn_hy_D, L1_attn_hy_fcD_w, L1_attn_hy_norm_w, L1_attn_hy_out_w, L1_ffn_gate_w, L1_ffn_gate_z, L1_ffn_gate_s, L1_ffn_up_w, L1_ffn_up_z, L1_ffn_up_s, L1_ffn_down_w, L1_ffn_down_z, L1_ffn_down_s):

    def _L0_attn_ref(hidden_states, Wq, Wk, Wv, Wo):
        import jax, jax.numpy as jnp
        import numpy as np
        B, S, HID = (2, 128, 512)
        N_HEADS, N_KV_HEADS = (32, 8)
        HEAD_DIM = HID // N_HEADS
        N_REP = N_HEADS // N_KV_HEADS
        ROPE_THETA = 10000.0

        def _rope(x, cos, sin):
            xe = x[..., 0::2]
            xo = x[..., 1::2]
            oe = xe * cos - xo * sin
            oo = xe * sin + xo * cos
            return jnp.stack([oe, oo], axis=-1).reshape(x.shape)
        b, s, _ = hidden_states.shape
        q = (hidden_states @ Wq.T).reshape(b, s, N_HEADS, HEAD_DIM).transpose(0, 2, 1, 3)
        k = (hidden_states @ Wk.T).reshape(b, s, N_KV_HEADS, HEAD_DIM).transpose(0, 2, 1, 3)
        v = (hidden_states @ Wv.T).reshape(b, s, N_KV_HEADS, HEAD_DIM).transpose(0, 2, 1, 3)
        pos = jnp.arange(s, dtype=jnp.float32)
        inv_freq = 1.0 / ROPE_THETA ** (jnp.arange(0, HEAD_DIM, 2, dtype=jnp.float32) / HEAD_DIM)
        freqs = pos[:, None] * inv_freq[None, :]
        cos, sin = (jnp.cos(freqs), jnp.sin(freqs))
        q = _rope(q, cos, sin)
        k = _rope(k, cos, sin)
        k = jnp.repeat(k, N_REP, axis=1)
        v = jnp.repeat(v, N_REP, axis=1)
        scores = jnp.einsum('bhsd,bhtd->bhst', q, k) / jnp.sqrt(jnp.float32(HEAD_DIM))
        causal = jnp.tril(jnp.ones((s, s), dtype=bool))
        scores = jnp.where(causal[None, None], scores, jnp.finfo(scores.dtype).min)
        attn = jax.nn.softmax(scores, axis=-1)
        out = jnp.einsum('bhst,bhtd->bhsd', attn, v)
        out = out.transpose(0, 2, 1, 3).reshape(b, s, HID)
        return out @ Wo.T

    def _L0_ffn_ref(x, gate_qweight, gate_scales, gate_zeros, up_qweight, up_scales, up_zeros, down_qweight, down_scales, down_zeros):
        import jax, jax.numpy as jnp
        import numpy as np
        HIDDEN = 512
        INTER = 1376
        GROUPSIZE = 128
        PACK = 8

        def dequant_gptq(qweight, scales, zeros, groupsize):
            K = qweight.shape[0] * PACK
            N = qweight.shape[1]
            k = jnp.arange(K)
            q = qweight[k // PACK, :] >> (k % PACK * 4)[:, None] & 15
            n = jnp.arange(N)
            z = zeros[:, n // PACK] >> (n % PACK * 4)[None, :] & 15
            s = scales.astype(jnp.float32)
            zp = (z.astype(jnp.float32) + 1.0) * s
            g = k // groupsize
            return q.astype(jnp.float32) * s[g] - zp[g]
        B, S, H = x.shape
        x2 = x.reshape(-1, H).astype(jnp.float32)
        Wg = dequant_gptq(gate_qweight, gate_scales, gate_zeros, GROUPSIZE)
        Wu = dequant_gptq(up_qweight, up_scales, up_zeros, GROUPSIZE)
        Wd = dequant_gptq(down_qweight, down_scales, down_zeros, GROUPSIZE)
        gate = x2 @ Wg
        up = x2 @ Wu
        inter = gate * jax.nn.sigmoid(gate) * up
        out = (inter @ Wd).astype(jnp.float16)
        return out.reshape(B, S, H)

    def _L1_attn_ref(x, w_down, b_down, w_up, b_up, gate1, hy_in_w, hy_conv_w, hy_conv_b, hy_dt_bias, hy_A_log, hy_D, hy_fcD_w, hy_norm_w, hy_out_w):
        import jax, jax.numpy as jnp
        import numpy as np
        HID = 512
        DM = 128
        DIN = 2 * DM
        DST = 16
        HD = 64
        NH = DIN // HD
        DCONV = 7
        CONV_DIM = DIN + 2 * DST
        DIN_PROJ = 2 * DIN + 2 * DST + 2 * NH
        SEQ, BATCH = (256, 4)

        def _causal_conv(x, w, b):
            y = jax.lax.conv_general_dilated(jnp.transpose(x, (0, 2, 1)), w, (1,), [(DCONV - 1, 0)], feature_group_count=CONV_DIM, dimension_numbers=('NCH', 'OIH', 'NCH'))
            return jnp.transpose(y, (0, 2, 1)) + b

        def _ssm_scan(x, dt, A, B, C):
            dA = jnp.exp(dt * A)
            dBx = dt[..., None] * x

            def step(h, t):
                dA_t, dBx_t, B_t, C_t = t
                h = dA_t[:, :, None, None] * h + dBx_t[..., None] * B_t[:, None, None, :]
                y = jnp.einsum('bhpn,bn->bhp', h, C_t)
                return (h, y)
            h0 = jnp.zeros((x.shape[0], NH, HD, DST), x.dtype)
            _, ys = jax.lax.scan(step, h0, (jnp.moveaxis(dA, 1, 0), jnp.moveaxis(dBx, 1, 0), jnp.moveaxis(B, 1, 0), jnp.moveaxis(C, 1, 0)))
            return jnp.moveaxis(ys, 0, 1)

        def _hydra(u, in_w, conv_w, conv_b, dt_bias, A_log, D, fcD_w, norm_w, out_w):
            b, l, _ = u.shape
            zxbcdt = u @ in_w.T
            z = zxbcdt[..., :DIN]
            xBC = zxbcdt[..., DIN:DIN + CONV_DIM]
            dt2 = zxbcdt[..., DIN + CONV_DIM:]
            dt_fw = jax.nn.softplus(dt2[..., :NH] + dt_bias)
            dt_bw = jax.nn.softplus(jnp.flip(dt2[..., NH:], 1) + dt_bias)
            xBC = jax.nn.silu(_causal_conv(xBC, conv_w, conv_b))
            xs = xBC[..., :DIN]
            Bm = xBC[..., DIN:DIN + DST]
            Cm = xBC[..., DIN + DST:]
            A = -jnp.exp(A_log)
            x4 = xs.reshape(b, l, NH, HD)
            y_fw = _ssm_scan(x4, dt_fw, A, Bm, Cm).reshape(b, l, DIN)
            y_bw = jnp.flip(_ssm_scan(jnp.flip(x4, 1), dt_bw, A, jnp.flip(Bm, 1), jnp.flip(Cm, 1)).reshape(b, l, DIN), 1)
            zero = jnp.zeros((b, 1, DIN), u.dtype)
            y = jnp.concatenate([zero, y_fw[:, :-1]], 1) + jnp.concatenate([y_bw[:, 1:], zero], 1)
            y = y + xs * jnp.repeat(xs @ fcD_w.T + D, HD, axis=-1)
            yz = y * jax.nn.silu(z)
            y = yz * jax.lax.rsqrt(jnp.mean(jnp.square(yz), -1, keepdims=True) + 1e-05) * norm_w
            return y @ out_w.T
        x_init = x
        h = x @ w_down.T + b_down
        h = jnp.transpose(h, (1, 0, 2))
        h = jax.nn.gelu(h, approximate=False)
        xmid = h
        hp = (hy_in_w, hy_conv_w, hy_conv_b, hy_dt_bias, hy_A_log, hy_D, hy_fcD_w, hy_norm_w, hy_out_w)
        h = _hydra(h, *hp)
        h = _hydra(h, *hp)
        alpha = jax.nn.sigmoid(gate1)
        h = alpha * xmid + (1.0 - alpha) * h
        h = xmid + h
        h = h @ w_up.T + b_up
        return x_init + jnp.transpose(h, (1, 0, 2))

    def _L1_ffn_ref(x, gate_w, gate_z, gate_s, up_w, up_z, up_s, down_w, down_z, down_s):
        import jax, jax.numpy as jnp
        import numpy as np
        GROUP_SIZE = 128

        def dequantize(imatrix, scales, zeros, group_size, out_dtype):
            rs = jnp.repeat(scales, group_size, axis=0)
            rz = jnp.repeat(zeros, group_size, axis=0)
            return ((imatrix.astype(rs.dtype) - rz.astype(rs.dtype)) * rs).astype(out_dtype)
        dt = x.dtype
        gate_proj = dequantize(gate_w, gate_s, gate_z, GROUP_SIZE, dt)
        up_proj = dequantize(up_w, up_s, up_z, GROUP_SIZE, dt)
        down_proj = dequantize(down_w, down_s, down_z, GROUP_SIZE, dt)
        gate = jax.nn.silu(jnp.dot(x, gate_proj))
        up = jnp.dot(x, up_proj)
        return jnp.dot(gate * up, down_proj)
    x = L0_attn_hidden_states
    x = _layernorm(x + _L0_attn_ref(x, L0_attn_Wq, L0_attn_Wk, L0_attn_Wv, L0_attn_Wo), axis=-1)
    x = _layernorm(x + _L0_ffn_ref(x, L0_ffn_gate_qweight, L0_ffn_gate_scales, L0_ffn_gate_zeros, L0_ffn_up_qweight, L0_ffn_up_scales, L0_ffn_up_zeros, L0_ffn_down_qweight, L0_ffn_down_scales, L0_ffn_down_zeros), axis=-1)
    x = _layernorm(x + _L1_attn_ref(x, L1_attn_w_down, L1_attn_b_down, L1_attn_w_up, L1_attn_b_up, L1_attn_gate1, L1_attn_hy_in_w, L1_attn_hy_conv_w, L1_attn_hy_conv_b, L1_attn_hy_dt_bias, L1_attn_hy_A_log, L1_attn_hy_D, L1_attn_hy_fcD_w, L1_attn_hy_norm_w, L1_attn_hy_out_w), axis=-1)
    x = _layernorm(x + _L1_ffn_ref(x, L1_ffn_gate_w, L1_ffn_gate_z, L1_ffn_gate_s, L1_ffn_up_w, L1_ffn_up_z, L1_ffn_up_s, L1_ffn_down_w, L1_ffn_down_z, L1_ffn_down_s), axis=-1)
    return x

_drawn_inputs = setup_inputs


def setup_inputs(seed=0):
    import zlib

    import numpy as np

    out = dict(_drawn_inputs(seed))
    spreads = {'L1_attn_b_down': (0.0, 0.642),
     'L1_attn_b_up': (0.0, 0.1),
     'L1_attn_hy_conv_b': (0.0, 0.8),
     'L1_attn_hy_D': (1.0, 0.6),
     'L1_attn_hy_norm_w': (1.0, 0.6)}
    factors = {'L0_attn_Wq': 8.0,
     'L0_attn_Wk': 8.0,
     'L1_attn_hy_in_w': 8.0,
     'L1_attn_hy_conv_w': 8.0,
     'L1_attn_hy_dt_bias': 8.0,
     'L1_attn_hy_A_log': 200.0,
     'L1_attn_hy_fcD_w': 8.0,
     'L1_attn_hy_out_w': 8.0}
    for name, (base, spread) in spreads.items():
        noise = np.random.default_rng([zlib.crc32(name.encode()), seed]).standard_normal(out[name].shape)
        drawn = base * np.exp(spread * noise) if base else spread * noise
        out[name] = jnp.asarray(drawn.astype(out[name].dtype))
    for name, factor in factors.items():
        out[name] = (out[name] * factor).astype(out[name].dtype)
    return out
```

```python
from contextlib import ExitStack

import numpy as np
import concourse.bass as bass
from concourse import mybir

F32 = mybir.dt.float32
F16 = mybir.dt.float16
BF16 = mybir.dt.bfloat16
I32 = mybir.dt.int32
ACT = mybir.ActivationFunctionType
ALU = mybir.AluOpType
AX = mybir.AxisListType.X

P = 128
NB, S, D = 4, 512, 512
NI = S // P
NT = NB * NI
KD = D // P
NH, NKV, HD = 32, 8, 16
NREP = NH // NKV
QKV = (NH + 2 * NKV) * HD
QK = (NH + NKV) * HD
VW = 34
W_SCALE = 256.0
INTER0, INTER1 = 1376, 1792
PACK = 8
DM, DIN, DST, NHY = 128, 256, 16, 4
CONV = DIN + 2 * DST
PROJ = 2 * DIN + 2 * DST + 2 * NHY
MASKED = -1e30
EPS = 1e-5


def bcast(ap, axis, n):
    shape = list(ap.shape)
    shape.insert(axis, n)
    return ap.unsqueeze(axis).broadcast_to(shape)


class Own:

    def __init__(self, eng, sem):
        self.eng, self.sem, self.base, self.n = eng, sem, 0, 0

    def did(self, ins):
        ins.then_inc(self.sem, 1)
        self.n += 1
        return self.base + self.n

    def wait(self, mark):
        self.eng.wait_ge(self.sem, mark)

    def link(self, ins):
        self.wait(self.did(ins))

    def enter(self, i, per):
        self.start, self.per = self.base + self.n, per
        self.base, self.n = self.start + i * per, 0

    def leave(self, times):
        assert self.n == self.per, f"steps of the loop's body: {self.n}, not {self.per}"
        self.base, self.n = self.start + times * self.per, 0


class Ffn:

    def __init__(self, inter):
        self.inter = inter
        self.tiles = [(f * P, min(P, inter - f * P)) for f in range(-(-inter // P))]
        self.n = len(self.tiles)


def units_of_batch():
    out = []
    for i in range(NI):
        w = (i + 1) * P
        g = 512 // w
        out += [(i, w, h, g) for h in range(0, NH, g)]
    return out


NLD1 = 16
DVE_LOOP = 109
POOL_LOOP = 44
DVE_FFN1 = 16


UNITS = units_of_batch()
NU = len(UNITS)
OG = 8
NOG = NH // OG
LAST = {i: max(n for n, u in enumerate(UNITS) if u[0] == i) for i in range(NI)}
OG_END = {}
for _n, (_i, _w, _h, _g) in enumerate(UNITS):
    if (_h + _g) % OG == 0:
        OG_END[_n] = _i * NOG + (_h + _g) // OG - 1


F0 = Ffn(INTER0)
NGU = 2 * F0.n
H2 = S // 2
G_AT = {1 + 2 * n * 4 // 3: n for n in range(NGU)}
U_AT = {1 + (2 * n + 1) * 4 // 3: n for n in range(NGU)}
OUT6 = [(LAST[i] + 7, LAST[i] + 11) for i in range(NI)]
G_SLOT = {n: u for u, n in G_AT.items()}
GU_BANK = {}
for _u, _n in sorted(G_AT.items()):
    _busy = any(lo - 2 <= _u <= hi for lo, hi in OUT6)
    GU_BANK[_n] = 7 if _busy or GU_BANK.get(_n - 1) == 6 else 6
GU_PREV = {n: max([m for m in range(n) if GU_BANK[m] == GU_BANK[n]], default=None) for n in range(NGU)}
DOWN0 = max(U_AT) + 3
DP = 5
DOWN_AT = {DOWN0 + (DP + 1) * i + k: (i, k) for i in range(NI) for k in range(DP)}
Y_AT = {DOWN0 + (DP + 1) * i + DP: i for i in range(NI)}
FTR_AT = {DOWN0 + 8 + 5 * i: i for i in range(NI - 1)}
UEND = NU + 17
W1C = 448
CHG = [(k, c) for k in "gu" for c in range(0, INTER1, W1C)]
ND1 = 3
NC1R = len(CHG) + ND1
W1_AT = {8 + 7 * c: c for c in range(NC1R)}


def build(nc, A):
    ctx = ExitStack()
    sems = {}

    def sem(name):
        if name not in sems:
            sems[name] = ctx.enter_context(nc.semaphore(name))
        return sems[name]

    def allocator(stack):
        return lambda name, shape, dt=F32: stack.enter_context(nc.sbuf_tensor(name, shape, dt))

    f0, f1 = Ffn(INTER0), Ffn(INTER1)
    with ctx:
        sb = allocator(ctx)
        ps = ctx.enter_context(nc.psum_tensor("ps", [P, 8, 512], F32))
        identf = sb("identf", [P, P])
        identh = sb("identh", [P, P], F16)
        identb = sb("identb", [P, P], BF16)
        mask = sb("mask", [P, P], BF16)
        neghalf = sb("neghalf", [P, 4])

        L = ExitStack()
        lb = allocator(L)
        w0 = {k: [lb(f"w0{k}{p}", [P, KD, INTER0] if k in "gu" else [P, f0.n, D], F16) for p in "hl"] for k in "gud"}
        shift = lb("shift", [P, 1], I32)
        costab = lb("costab", [P, NI, HD])
        sintab = lb("sintab", [P, NI, HD])
        wqkv = lb("wqkv", [P, KD, QKV])
        wo = lb("wo", [P, KD, D])
        xin = lb("xin", [P, NI, D])
        V = lb("V", [P, NI, NKV, VW], F16)
        Pe = lb("Pe", [P, 2, 512])
        pth = lb("pth", [P, 3, 512], F16)
        ptl = lb("ptl", [P, 3, 512], F16)
        nmax = lb("nmax", [P, 4, 4])
        osum = lb("osum", [P, OG, HD])
        rinv = lb("rinv", [P, OG])
        attn = lb("attn", [P, 2, D])
        aT = lb("aT", [P, KD, P])
        st6 = lb("st6", [P, 6])
        mv = lb("mv", [P, 2, 2])
        ve = lb("ve", [P, 2])
        rstd = lb("rstd", [P, 2])
        st6b = lb("st6b", [P, 6])
        mvb = lb("mvb", [P, 2, 2])
        veb = lb("veb", [P, 2])
        rstdb = lb("rstdb", [P, 2])
        qT = lb("qT", [P, NH // 2, S], F16)
        kT = lb("kT", [P, NKV * 2, S], F16)
        LI = ExitStack()
        li = allocator(LI)
        int0 = [li(f"int0{p}", [P, f0.n, S], F16) for p in "hl"]
        LI.close()
        xT = lb("xT", [P, 2, KD, P])
        qk_c = lb("qk_c", [P, QK])
        qk_s = lb("qk_s", [P, QK])
        qk = lb("qk", [P, 2, QK])
        stq = lb("stq", [P, NH, 4, HD], F16)
        stk = lb("stk", [P, NKV, 2, 2, 4, HD], F16)
        HW = INTER0 // 2
        LS = ExitStack()
        ls = allocator(LS)
        wv = ls("wv", [P, HW])
        pk = ls("pk", [P, 2, HW], I32)
        zb = ls("zb", [P, 2, HW], F16)
        nib = ls("nib", [P, 2, HW], I32)
        zk = ls("zk", [16, 172], I32)
        zi = ls("zi", [16, INTER0], I32)
        zs = ls("zs", [16, INTER0], F16)
        LS.close()
        x1r = lb("x1r", [P, NI, D])
        sg = lb("sg", [P, 2, H2])
        prod = lb("prod", [P, 2, H2])
        y16 = lb("y16", [P, 2, D], F16)
        vq = lb("vq", [P, 512])
        vz = lb("vz", [P, 512], I32)
        vs = lb("vs", [P, 512])
        vh = lb("vh", [P, 512], F16)
        vl = lb("vl", [P, 512], F16)
        x1 = lb("x1", [P, NI, D])
        xh = lb("xh", [P, KD, S], F16)
        xl = lb("xl", [P, KD, S], F16)
        L.close()

        C = ExitStack()
        cb = allocator(C)
        w1 = {k: [cb(f"w1{k}{p}", [P, KD, INTER1] if k in "gu" else [P, f1.n, D], F16) for p in "hl"] for k in "gud"}
        CH = ExitStack()
        ch = allocator(CH)
        xc = ch("xc", [P, NI, NB, CONV])
        zg = ch("zg", [P, NI, NB, DIN])
        CH.close()
        CH2 = ExitStack()
        ch2 = allocator(CH2)
        x2a = ch2("x2a", [P, NI, D])
        xTb = ch2("xTb", [P, KD, S])
        CH2.close()
        x3h = cb("x3h", [P, KD, NT * P], F16)
        x3l = cb("x3l", [P, KD, NT * P], F16)
        pad3 = cb("pad_h", [P, 512])
        CX = ExitStack()
        cx = allocator(CX)
        xraw = cx("xraw", [P, NB, CONV])
        yy = cx("yy", [P, NB, DIN])
        ty = cx("ty", [P, NB, DIN])
        yp = cx("yp", [P, NB, DIN])
        CX.close()
        x3 = cb("x3", [P, NT, D])
        CI = ExitStack()
        ci = allocator(CI)
        int1 = [ci(f"int1{p}", [P, f1.n, S], F16) for p in "hl"]
        sg1 = ci("sg1", [P, 2, S])
        prod1 = ci("prod1", [P, 2, S])
        ob = ci("ob", [P, 2, D])
        CI.close()
        uT = cb("uT", [P, NB, S])
        xmid = cb("xmid", [P, NB, S])
        cscr = cb("cscr", [P, 4, D])
        yT = cb("yT", [P, 2, S])
        inwT = cb("inwT", [P, PROJ])
        owT = cb("owT", [P, 2, DM])
        wdT = cb("wdT", [P, KD, DM])
        wuT = cb("wuT", [P, D])
        bup = cb("bup", [P, D])
        convw = cb("convw", [P, NB, CONV])
        convb = cb("convb", [P, CONV])
        fcD = cb("fcD", [P, NHY, DIN])
        dtr = cb("dtr", [P, NT, 2 * NHY])
        sm = {n: cb(f"sm_{n}", [P, NT, 2 * NHY]) for n in ("v", "e", "mx", "w", "w2", "p", "dt", "da")}
        CB = cb("CB", [P, NI, 16])
        Rf = cb("Rf", [P, NI, 3, 3, NHY])
        Sb = cb("Sb", [P, NI, 3, 3, NHY])
        M = cb("M", [P, NI, NB, NB, NHY])
        Fd = cb("Fd", [P, NI, NB, NHY])
        ss = cb("ss", [P, NI, NB])
        rs = cb("rs", [P, NI, NB])
        A8 = cb("A8", [P, 2 * NHY])
        dtb8 = cb("dtb8", [P, 2 * NHY])
        D4 = cb("D4", [P, NHY])
        nw = cb("nw", [P, 2])
        bdn = cb("bdn", [P, 1])
        al = cb("al", [P, 4])
        st6c = cb("st6c", [P, 6])
        mvc = cb("mvc", [P, 2, 2])
        vec = cb("vec", [P, 2])
        rstdc = cb("rstdc", [P, 2])
        C.close()

        zs_dram = {k: nc.dram_tensor(f"zs_{k}", [16, INTER0], F16, kind="Internal").ap() for k in "gud"}
        x2_dram = nc.dram_tensor("x2_dram", [NT, P, D], F32, kind="Internal").ap()
        w1_dram = {k: [nc.dram_tensor(f"w1_{k}{p}", [KD, P, INTER1] if k in "gu" else [f1.n, P, D], F16, kind="Internal").ap() for p in "hl"]
                   for k in "gud"}
        w1_rows = {k: A[f"q1{k}"].rearrange("(g p) n -> g p n", p=P) for k in "gud"}

        x_rows = A["x"].rearrange("b (i p) d -> b p i d", p=P)
        block = ctx.enter_context(nc.Block())
        CH0 = [(k, g, c, HW) for k in "gu" for g in range(KD) for c in (0, HW)]
        CH0 += [("d", g, 0, D) for g in range(f0.n)]
        NC0 = len(CH0)
        def w1_chunk(b, c):
            if c < len(CHG):
                k, c0 = CHG[c]
                return k, b, slice(c0, c0 + W1C), W1C
            return "d", ND1 * b + c - len(CHG), slice(0, D), D

        def one(ap, g, cols):
            return ap[bass.ds(g, 1), :, cols].rearrange("o p n -> (o p) n")

        NC1 = NC1R * NB + f1.n - ND1 * NB

        def gu_bank(b, n):
            return GU_BANK[n] if b is not None else 6 + n % 2

        def down_bank(b, i):
            return 7 if b is not None else 6 + i % 2

        def rows0(k, g):
            return min(P, INTER0 - g * P) if k == "d" else P

        t1 = yy[:, :, :].rearrange("p a b -> p (a b)")[:, 0:3 * CONV].rearrange("p (l c) -> p l c", l=3)
        t2 = ty[:, :, :].rearrange("p a b -> p (a b)")[:, 0:2 * CONV].rearrange("p (l c) -> p l c", l=2)
        t3 = yp[:, :, :].rearrange("p a b -> p (a b)")[:, 0:CONV].rearrange("p (l c) -> p l c", l=1)
        conv_t = {1: t1, 2: t2, 3: t3}
        cscr_flat = cscr[:, :, :].rearrange("p a b -> p (a b)")
        yc = cscr_flat[:, 0:NB * CONV].rearrange("p (l c) -> p l c", l=NB)
        junk = cscr_flat[:, 1152:1152 + 768].rearrange("p (a b) -> p a b", a=3)

        def xs_b(st, m):
            return bcast(xc[:, st, m, 0:DIN].rearrange("p (h c) -> p h c", h=NHY), 1, NB)

        def m_b(st, m):
            return bcast(M[:, st, :, m, :], 3, DIN // NHY)

        def w1_load(sp, c, k, g, cols, n):
            sp.wait_ge(sem("w1_lo"), c)
            sp.sem_inc(sem("sp_seen"), 1)
            sp.dma_start(vq[:, 0:n].bitcast(I32), one(w1_rows[k], g, cols)).then_inc(sem("ld_w1c"), 16)
            sp.dma_start(vz[:, 0:n], A[f"z1{k}"][bass.ds(g, 1), cols].rearrange("o n -> (o n)").partition_broadcast(P)).then_inc(sem("ld_w1c"), 16)
            sp.dma_start(vs[:, 0:n], A[f"s1{k}"][bass.ds(g, 1), cols].rearrange("o n -> (o n)").partition_broadcast(P)).then_inc(sem("ld_w1c"), 16)

        def w1_store(sp, c, k, g, cols, n):
            sp.wait_ge(sem("w1_lo"), c + 1)
            sp.sem_inc(sem("sp_seen"), 1)
            sp.dma_start(one(w1_dram[k][0], g, cols), vh[:, 0:n]).then_inc(sem("st_w1"), 16)
            sp.dma_start(one(w1_dram[k][1], g, cols), vl[:, 0:n]).then_inc(sem("st_w1"), 16)

        def sp_round(sp, b, more):
            for c in range(NC1R + 1):
                if c < NC1R:
                    w1_load(sp, NC1R * b + c, *w1_chunk(b, c))
                if c:
                    w1_store(sp, NC1R * b + c - 1, *w1_chunk(b, c - 1))
            if more:
                sp.wait_ge(sem("x1_sum"), NI * b + NI)
                sp.sem_inc(sem("sp_seen"), 1)
                sp.dma_start(xin[:, :, :], x_rows[bass.ds(b + 1, 1)].rearrange("o p i d -> (o p) i d")).then_inc(sem("ld_x"), 16)

        @block.sync
        def _(sp):
            sp.dma_start(shift[:, :], A["shift"]).then_inc(sem("ld_shift"), 16)
            for n, k in enumerate("gud"):
                G, N8 = (KD, INTER0 // PACK) if k in "gu" else (f0.n, D // PACK)
                if n:
                    sp.wait_ge(sem("zk_done"), n)
                sp.dma_start(zk[0:G, 0:N8], A[f"z0{k}"]).then_inc(sem("ld_zk"), 16)
                sp.wait_ge(sem("zs_done"), n + 1)
                sp.dma_start(zs_dram[k][0:G, 0:N8 * PACK], zs[0:G, 0:N8 * PACK]).then_inc(sem("st_zs"), 16)
                if n == 0:
                    sp.dma_start(xin[:, :, :], x_rows[0]).then_inc(sem("ld_x"), 16)
                    for name, t in (("wqkvT", wqkv), ("woT", wo)):
                        sp.dma_start(t[:, :, :], A[name].rearrange("(k p) n -> p k n", p=P)).then_inc(sem("ld_wa"), 16)
                    sp.dma_start(costab[:, :, :], A["cos"].rearrange("(i p) n -> p i n", p=P)).then_inc(sem("ld_wa"), 16)
                    sp.dma_start(sintab[:, :, :], A["sin"].rearrange("(i p) n -> p i n", p=P)).then_inc(sem("ld_wa"), 16)
            for c, (k, g, c0, n) in enumerate(CH0):
                r = rows0(k, g)
                mi = "gud".index(k)
                sp.wait_ge(sem("st_zs"), 16 * (mi + 1))
                if c >= 2:
                    sp.wait_ge(sem("deq_d"), c - 1)
                src = bcast(A[f"q0{k}"][g * 16:g * 16 + r // PACK, c0:c0 + n], 1, PACK)
                sp.dma_start(pk[0:r, c % 2, 0:n], src).then_inc(sem(f"ld_pk{c % 2}"), 16)
                sp.dma_start(zb[0:r, c % 2, 0:n], zs_dram[k][g, c0:c0 + n].partition_broadcast(r)).then_inc(sem(f"ld_pk{c % 2}"), 16)
                sp.dma_start(w0[k][1][0:r, g, c0:c0 + n], A[f"s0{k}"][g, c0:c0 + n].partition_broadcast(r)).then_inc(sem(f"ld_pk{c % 2}"), 16)
            sp.wait_ge(sem("w0_ready"), 1)
            sp_round(sp, 0, True)
            with sp.Fori(0, NB - 2) as f:
                sp_round(sp, f + 1, True)
            sp_round(sp, NB - 1, False)
            for g in range(ND1 * NB, f1.n):
                c = NC1R * NB + g - ND1 * NB
                w1_load(sp, c, "d", g, slice(0, D), D)
                w1_store(sp, c, "d", g, slice(0, D), D)
            sp.wait_ge(sem("loop_act"), 1)
            sp.wait_ge(sem("loop_dve"), 1)
            sp.wait_ge(sem("loop_pe"), 1)
            sp.wait_ge(sem("loop_pool"), 1)
            sp.wait_ge(sem("st_x2"), 16 * NT)
            ld = []
            ld.append((inwT[:, :], A["inwT"]))
            ld.append((owT[:, :, :], A["owT"].rearrange("(k p) n -> p k n", p=P)))
            ld.append((wdT[:, :, :], A["wdT"].rearrange("(k p) n -> p k n", p=P)))
            ld.append((wuT[:, :], A["wuT"]))
            ld.append((bup[:, :], A["bup"].partition_broadcast(P)))
            ld.append((convw[:, :, :], A["convw"].partition_broadcast(P)))
            ld.append((convb[:, :], A["convb"].partition_broadcast(P)))
            ld.append((fcD[:, :, :], A["fcD"].partition_broadcast(P)))
            for half in range(2):
                ld.append((A8[:, half * NHY:half * NHY + NHY], A["Alog"].partition_broadcast(P)))
                ld.append((dtb8[:, half * NHY:half * NHY + NHY], A["dtb"].partition_broadcast(P)))
            ld.append((D4[:, :], A["D"].partition_broadcast(P)))
            ld.append((nw[:, :], A["nw"]))
            ld.append((bdn[:, :], A["bdn"].rearrange("(p o) -> p o", o=1)))
            ld.append((al[:, 0:1], A["gate"].partition_broadcast(P)))
            assert len(ld) == NLD1
            for dst, src in ld:
                sp.dma_start(dst, src).then_inc(sem("ld_w1"), 16)
            for l in range(NB):
                if l:
                    sp.wait_ge(sem("c1_tr"), NI * l)
                sp.dma_start(x2a[:, :, :], x2_dram[NI * l:NI * l + NI].rearrange("i p d -> p i d")).then_inc(sem("ld_x2"), 16)
            sp.wait_ge(sem("st_w1"), 32 * NC1)
            for k in "gud":
                for part in range(2):
                    sp.dma_start(w1[k][part][:, :, :], w1_dram[k][part].rearrange("g p n -> p g n")).then_inc(sem("ld_wf"), 16)
            for t in range(NT):
                if t >= 4:
                    sp.wait_ge(sem("x3_sum"), t - 3)
                else:
                    sp.wait_ge(sem("hT"), NB)
                sp.dma_start(cscr[:, t % 4, :], x2_dram[t]).then_inc(sem(f"ld_x2r{t % 4}"), 16)
            with sp.Fori(0, NB) as b:
                for i in range(NI):
                    sp.wait_ge(sem("out_ready"), NI * b + i + 1)
                    sp.dma_start(A["out"][bass.ds(b, 1), i * P:(i + 1) * P, :].rearrange("o p d -> (o p) d"), ob[:, i % 2, :]).then_inc(sem(f"st_out{i % 2}"), 16)
            for r in range(2):
                sp.wait_ge(sem(f"st_out{r}"), 16 * NT // 2)

        def ffn_pool(pool, b, f, s, prod_, inter):
            for j, (_, n) in enumerate(f.tiles):
                pool.wait_ge(sem(s + "_hi"), f.n * b + j + 1)
                pool.tensor_tensor(inter[1][0:n, j, :], prod_[0:n, j % 2, :], inter[0][0:n, j, :], ALU.subtract).then_inc(sem(s + "_lo"), 1)

        def w1_prep(pool, own, c, n):
            pool.wait_ge(sem("ld_w1c"), 48 * (c + 1))
            q, z, hi, lo = (t[:, 0:n] for t in (vq, vz, vh, vl))
            own.link(pool.tensor_tensor(q.bitcast(I32), q.bitcast(I32), z, ALU.subtract))
            pool.sem_inc(sem("w1_i"), 1)
            own.link(pool.tensor_scalar(q, q.bitcast(I32), W_SCALE, 0.0, ALU.mult, ALU.add))
            own.link(pool.tensor_tensor(q, q, vs[:, 0:n], ALU.mult))
            pool.sem_inc(sem("w1_i"), 1)
            pool.wait_ge(sem("st_w1"), 32 * c)
            pool.sem_inc(sem("w1_i"), 1)
            own.link(pool.tensor_scalar(hi, q, 1.0, 0.0, ALU.mult, ALU.add))
            pool.tensor_tensor(lo, q, hi, ALU.subtract).then_inc(sem("w1_lo"), 1)

        def round_pool(pool, own, b, f):
            if b is not None and f is not None:
                pool.wait_ge(sem("fxl"), NI * b)
                pool.sem_inc(sem("stk_free"), 1)
                pool.memset(stk[:, :, 0, 1, :, :], 0.0)
                pool.memset(stk[:, :, 1, 0, :, :], 0.0).then_inc(sem("stk_zero"), 1)
            for u in range(UEND):
                if b is not None:
                    if u in W1_AT:
                        c = W1_AT[u]
                        w1_prep(pool, own, NC1R * b + c, w1_chunk(b, c)[3])
                    for i in range(NI):
                        if u == LAST[i] + 12:
                            pool.wait_ge(sem("ve1"), NI * b + i + 1)
                            pool.tensor_tensor(rstd[:, i % 2:i % 2 + 1], ve[:, i % 2:i % 2 + 1], neghalf[:, 0:1], ALU.pow).then_inc(sem("rstd1"), 1)
                if f is not None:
                    if u - 3 in U_AT:
                        n = U_AT[u - 3]
                        j, half = divmod(n, 2)
                        r, cols = f0.tiles[j][1], slice(half * H2, half * H2 + H2)
                        pool.wait_ge(sem("f0_hi"), NGU * f + n + 1)
                        pool.tensor_tensor(int0[1][0:r, j, cols], prod[0:r, n % 2, :], int0[0][0:r, j, cols], ALU.subtract).then_inc(sem("f0_lo"), 1)
                    if u - 1 in Y_AT:
                        i = Y_AT[u - 1]
                        pool.wait_ge(sem("ve2"), NI * f + i + 1)
                        pool.tensor_tensor(rstdb[:, i % 2:i % 2 + 1], veb[:, i % 2:i % 2 + 1], neghalf[:, 0:1], ALU.pow).then_inc(sem("rstd2"), 1)
                        pool.wait_ge(sem("x2_done"), NI * f + i + 1)
                        pool.dma_start(x2_dram[bass.ds(NI * f + i, 1)].rearrange("o p d -> (o p) d"), x1r[:, i, :]).then_inc(sem("st_x2"), 16)

        def layer1_pool(pool):
            pool.wait_ge(sem("loop_act"), 1)
            pool.wait_ge(sem("loop_dve"), 1)
            pool.wait_ge(sem("loop_pe"), 1)
            for p in range(2):
                for st in range(NI):
                    pool.wait_ge(sem("h_raw"), NI * p + st + 1)
                    for j in (1, 2, 3):
                        ins = pool.tensor_tensor(conv_t[j], xraw[:, 0:NB - j, :], bcast(convw[:, 3 - j, :], 1, NB - j), ALU.mult)
                    ins.then_inc(sem("h_taps"), 1)
                for st in range(NI):
                    pool.wait_ge(sem("h_M"), NI * p + st + 1)
                    pool.tensor_tensor(yp[:, :, :].rearrange("p l (h c) -> p l h c", h=NHY), xs_b(st, 3), m_b(st, 3), ALU.mult).then_inc(sem("h_yp"), 1)
                    pool.wait_ge(sem("h_ss"), NI * p + st + 1)
                    v = rs[:, st, :]
                    pool.tensor_scalar(v, ss[:, st, :], 1.0 / DIN, EPS, ALU.mult, ALU.add).then_inc(sem("h_ve"), 1)
                    pool.wait_ge(sem("h_ve"), NI * p + st + 1)
                    pool.tensor_tensor(v, v, neghalf[:, :], ALU.pow).then_inc(sem("h_rs"), 1)
            for t in range(NT):
                pool.wait_ge(sem("ve3"), t + 1)
                pool.tensor_tensor(rstdc[:, t % 2:t % 2 + 1], vec[:, t % 2:t % 2 + 1], neghalf[:, 0:1], ALU.pow).then_inc(sem("rstd3"), 1)
            with pool.Fori(0, NB) as b:
                ffn_pool(pool, b, f1, "f1", prod1, int1)
                for i in range(NI):
                    pool.wait_ge(sem("ve4"), NI * b + i + 1)
                    pool.tensor_tensor(rstdc[:, i % 2:i % 2 + 1], vec[:, i % 2:i % 2 + 1], neghalf[:, 0:1], ALU.pow).then_inc(sem("rstd4"), 1)

        @block.gpsimd
        def _(pool):
            own = Own(pool, sem("own_pool"))
            own.did(pool.memset(identf[:, :], 0.0))
            own.did(pool.memset(identh[:, :], 0.0))
            own.did(pool.memset(identb[:, :], 0.0))
            own.link(pool.memset(mask[:, :], 0.0))
            for t in (identf, identh, identb):
                own.did(pool.affine_select(out=t[:, :], in_=t[:, :], compare_op=ALU.not_equal, fill=1.0, base=0,
                                           pattern=[[-1, P]], channel_multiplier=1))
            own.did(pool.affine_select(out=mask[:, :], in_=mask[:, :], compare_op=ALU.is_ge, fill=MASKED, base=0,
                                       pattern=[[-1, P]], channel_multiplier=1))
            own.did(pool.memset(neghalf[:, :], -0.5))
            own.did(pool.memset(V[:, :, :, 2 * HD + 1:VW], 0.0))
            own.did(pool.memset(stk[:, :, :, :, :, :], 0.0))
            own.link(pool.memset(V[:, :, :, 2 * HD:2 * HD + 1], 1.0))
            pool.sem_inc(sem("consts"), 1)
            for c, (k, g, c0, n) in enumerate(CH0):
                r = rows0(k, g)
                hi, lo = (w0[k][p][0:r, g, c0:c0 + n] for p in (0, 1))
                pool.wait_ge(sem("deq_d"), c + 1)
                own.link(pool.tensor_tensor(wv[0:r, 0:n], hi, lo, ALU.mult))
                own.link(pool.tensor_scalar(hi, wv[0:r, 0:n], 1.0, 0.0, ALU.mult, ALU.add))
                own.link(pool.tensor_tensor(lo, wv[0:r, 0:n], hi, ALU.subtract))
            pool.sem_inc(sem("w0_ready"), 1)
            round_pool(pool, own, 0, None)
            with pool.Fori(0, NB - 1) as f:
                own.enter(f, POOL_LOOP)
                round_pool(pool, own, f + 1, f)
                own.leave(NB - 1)
            for g in range(ND1 * NB, f1.n):
                w1_prep(pool, own, NC1R * NB + g - ND1 * NB, D)
            round_pool(pool, own, None, NB - 1)
            pool.sem_inc(sem("loop_pool"), 1)
            layer1_pool(pool)

        def stage_act(act, b, i):
            act.wait_ge(sem("qk"), NI * b + i + 1)
            if i:
                act.wait_ge(sem("str"), 4 * NI * b + 4 * i)
            q = qk[:, i % 2, 0:NH * HD].rearrange("p (h c) -> p h c", h=NH)
            k = qk[:, i % 2, NH * HD:QK].rearrange("p (h c) -> p h c", h=NKV)
            act.activation(stq[:, :, 0:4:2, :], bcast(q, 2, 2), ACT.Copy, scale=HD ** -0.5)
            act.activation(stk[:, :, 0, 0, 0:2, :], bcast(k, 2, 2), ACT.Copy)
            act.activation(stk[:, :, 1, 1, 0:2, :], bcast(k, 2, 2), ACT.Copy)
            vp = ps[:, 1 + 2 * (i % 2), QK - 512:QKV - 512].rearrange("p (g c) -> p g c", g=NKV)
            act.activation(V[:, i, :, 0:HD], vp, ACT.Copy).then_inc(sem("st_hi"), 1)
            for gi in (0, 2):
                act.wait_ge(sem("str"), 4 * NI * b + 4 * i + gi + 1)
                dst = (qT if gi < 2 else kT)[:, 0:8, i * P:(i + 1) * P]
                act.activation(dst, ps[:, 4, :].bitcast(F16).rearrange("p (a n) -> p a n", a=8), ACT.Copy).then_inc(sem("ste_act"), 1)

        def ffn_act(act, b, f, s, sg_, prod_, inter):
            for j in range(f.n + 1):
                if j < f.n:
                    n = f.tiles[j][1]
                    act.wait_ge(sem(s + "_gu"), f.n * b + j + 1)
                    if j >= 2:
                        act.wait_ge(sem(s + "_prod"), f.n * b + j - 1)
                    act.activation(sg_[0:n, j % 2, :], ps[0:n, j % 2, :], ACT.Silu, scale=1.0 / W_SCALE).then_inc(sem(s + "_sg"), 1)
                if j >= 1:
                    n = f.tiles[j - 1][1]
                    act.wait_ge(sem(s + "_prod"), f.n * b + j)
                    act.activation(inter[0][0:n, j - 1, :], prod_[0:n, (j - 1) % 2, :], ACT.Copy).then_inc(sem(s + "_hi"), 1)

        def projections_act(act, b):
            for i in range(NI):
                act.wait_ge(sem("xtr"), NI * b + i + 1)
                if i >= 2:
                    act.wait_ge(sem("proj"), NI * b + i - 1)
                act.activation(xT[:, i % 2, :, :].rearrange("p k n -> p (k n)"), ps[:, 6 + i % 2, :], ACT.Copy).then_inc(sem("xte"), 1)
                if i >= 1:
                    stage_act(act, b, i - 1)
            stage_act(act, b, NI - 1)

        def ffn0_input_act(act, b, i):
            act.wait_ge(sem("ftr"), NI * b + i + 1)
            act.activation(xh[:, :, i * P:(i + 1) * P], ps[:, 6, :].rearrange("p (k n) -> p k n", k=KD), ACT.Copy).then_inc(sem("fxh"), 1)

        def round_act(act, b, f):
            if b is not None:
                projections_act(act, b)
            for u in range(UEND):
                if f is not None and u - 1 in U_AT:
                    n = U_AT[u - 1]
                    r = f0.tiles[n // 2][1]
                    act.wait_ge(sem("f0_gu"), NGU * f + n + 1)
                    if n >= 2:
                        act.wait_ge(sem("f0_prod"), NGU * f + n - 1)
                    act.activation(sg[0:r, n % 2, :], ps[0:r, gu_bank(b, n), 0:H2], ACT.Tanh, scale=0.5 / W_SCALE).then_inc(sem("f0_sg"), 1)
                if b is not None:
                    if 2 <= u <= NU + 1:
                        v = u - 2
                        i, w, h0, g = UNITS[v]
                        act.wait_ge(sem("ptr"), NU * b + v + 1)
                        if v >= 3:
                            act.wait_ge(sem("pv"), NU * b + v - 2)
                        act.activation(pth[:, v % 3, 0:g * w], ps[:, 2 + v % 2, 0:g * w], ACT.Copy).then_inc(sem("pth"), 1)
                    if u < NU:
                        i, w, h0, g = UNITS[u]
                        act.wait_ge(sem("nmax"), NU * b + u + 1)
                        if u >= 2:
                            act.wait_ge(sem("ptr"), NU * b + u - 1)
                        for x in range(g):
                            ins = act.activation(Pe[:, u % 2, x * w:(x + 1) * w], ps[:, u % 2, x * w:(x + 1) * w], ACT.Exp,
                                                 bias=nmax[:, u % 4, x:x + 1])
                        ins.then_inc(sem("exp"), 1)
                    for i in range(NI):
                        if u == LAST[i] + 8:
                            act.wait_ge(sem("atr"), NI * b + i + 1)
                            act.activation(aT[:, :, :].rearrange("p k n -> p (k n)"), ps[:, 6, :], ACT.Copy).then_inc(sem("ate"), 1)
                    if u - 1 in FTR_AT:
                        ffn0_input_act(act, b, FTR_AT[u - 1])
                if f is not None:
                    if u - 3 in U_AT:
                        n = U_AT[u - 3]
                        j, half = divmod(n, 2)
                        r = f0.tiles[j][1]
                        act.wait_ge(sem("f0_prod"), NGU * f + n + 1)
                        act.activation(int0[0][0:r, j, half * H2:half * H2 + H2], prod[0:r, n % 2, :], ACT.Copy).then_inc(sem("f0_hi"), 1)
                    if u in Y_AT:
                        i = Y_AT[u]
                        act.wait_ge(sem("f0_down"), NI * f + i + 1)
                        if i >= 2:
                            act.wait_ge(sem("x2_sum"), NI * f + i - 1)
                        act.activation(y16[:, i % 2, :], ps[:, down_bank(b, i), :], ACT.Copy, scale=1.0 / W_SCALE).then_inc(sem("y16"), 1)
            if b is not None:
                ffn0_input_act(act, b, NI - 1)

        def layer1_act(act):
            act.wait_ge(sem("loop_dve"), 1)
            act.wait_ge(sem("loop_pe"), 1)
            act.wait_ge(sem("loop_pool"), 1)
            act.wait_ge(sem("ld_w1"), 16 * NLD1)
            act.wait_ge(sem("alog"), 1)
            act.activation(A8[:, :], A8[:, :], ACT.Exp)
            act.activation(al[:, 1:2], al[:, 0:1], ACT.Exp, scale=-1.0).then_inc(sem("c_exp"), 1)
            for l in range(NB):
                for i in range(NI):
                    act.wait_ge(sem("c1_tr"), NI * l + i + 1)
                    if i == 0 and l:
                        act.wait_ge(sem("c1_dn"), l)
                    act.activation(xTb[:, :, i * P:(i + 1) * P], ps[:, i, :].rearrange("p (k n) -> p k n", k=KD), ACT.Copy).then_inc(sem("c1_te"), 1)
                act.wait_ge(sem("c1_dn"), l + 1)
                act.activation(xmid[:, l, :], ps[:, 4 + l % 2, :], ACT.Gelu, bias=bdn[:, 0:1]).then_inc(sem("xmid"), 1)

            for p in range(2):
                for st in range(NI):
                    act.wait_ge(sem("h_in"), NI * p + st + 1)
                    if st or p:
                        act.wait_ge(sem("h_taps"), NI * p + st)
                        act.wait_ge(sem("h_conv"), NI * p + st)
                    act.activation(zg[:, st, :, :], ps[:, 0:NB, 0:DIN], ACT.Silu)
                    act.activation(xraw[:, :, 0:DIN], ps[:, 0:NB, DIN:2 * DIN], ACT.Copy)
                    bc = ps[:, 4 + st % 2, 0:NB * 64].rearrange("p (l c) -> p l c", l=NB)
                    act.activation(dtr[:, NI * st:NI * st + NB, :], bc[:, :, 2 * DST:2 * DST + 2 * NHY], ACT.Copy)
                    act.activation(xraw[:, :, DIN:CONV], bc[:, :, 0:2 * DST], ACT.Copy).then_inc(sem("h_raw"), 1)
                    act.wait_ge(sem("h_conv"), NI * p + st + 1)
                    act.activation(xc[:, st, :, :], yc, ACT.Silu).then_inc(sem("h_x"), 1)
                act.wait_ge(sem("h_v"), p + 1)
                act.activation(sm["e"][:, :, :], sm["e"][:, :, :], ACT.Exp, scale=-1.0).then_inc(sem("h_e"), 1)
                act.wait_ge(sem("h_adt"), p + 1)
                act.activation(sm["da"][:, :, :], sm["da"][:, :, :], ACT.Exp).then_inc(sem("h_da"), 1)
                for st in range(NI):
                    act.wait_ge(sem("h_y"), NI * p + st + 1)
                    for l in range(NB):
                        ins = act.activation(ty[:, l, :], yy[:, l, :], ACT.Square, accum_out=ss[:, st, l:l + 1])
                    ins.then_inc(sem("h_ss"), 1)
                    act.wait_ge(sem("h_ytr"), NI * p + st + 1)
                    act.activation(yT[:, :, :], ps[:, 4:6, :], ACT.Copy).then_inc(sem("h_yT"), 1)
            for t in range(NT):
                act.wait_ge(sem("x3tr"), t + 1)
                act.activation(x3h[:, :, t * P:(t + 1) * P], ps[:, 4 + t % 2, :].rearrange("p (k n) -> p k n", k=KD), ACT.Copy).then_inc(sem("x3h"), 1)
            with act.Fori(0, NB) as b:
                ffn_act(act, b, f1, "f1", sg1, prod1, int1)

        @block.scalar
        def _(act):
            act.wait_ge(sem("consts"), 1)
            round_act(act, 0, None)
            with act.Fori(0, NB - 1) as f:
                round_act(act, f + 1, f)
            round_act(act, None, NB - 1)
            act.sem_inc(sem("loop_act"), 1)
            layer1_act(act)

        def layer_norm_1(dve, own, r, st, m, v, ready):
            own.link(dve.bn_stats(st[:, :], r))
            dve.sem_inc(sem("bn"), 1)
            own.link(dve.bn_aggr(m, st[:, :]))
            dve.tensor_scalar(v, m[:, 1:2], EPS, None, ALU.add).then_inc(ready, 1)

        def rope(dve, own, b, i):
            dve.wait_ge(sem("proj"), NI * b + i + 1)
            base = 2 * (i % 2)
            src = ps[:, base:base + 2, :].rearrange("p k n -> p (k n)")[:, 0:QK].rearrange("p (h c t) -> p h c t", h=NH + NKV, t=2)
            cs, sn = (t[:, i, :] for t in (costab, sintab))
            d_c = qk_c[:, :].rearrange("p (h c) -> p h c", h=NH + NKV)
            d_s = qk_s[:, :].rearrange("p (h c t) -> p h c t", h=NH + NKV, t=2)
            own.did(dve.tensor_tensor(d_c, src.rearrange("p h c t -> p h (c t)"), bcast(cs, 1, NH + NKV), ALU.mult))
            s2 = sn.rearrange("p (c t) -> p c t", t=2)
            own.did(dve.tensor_tensor(d_s[:, :, :, 0], src[:, :, :, 1], bcast(s2[:, :, 0], 1, NH + NKV), ALU.mult))
            own.link(dve.tensor_tensor(d_s[:, :, :, 1], src[:, :, :, 0], bcast(s2[:, :, 1], 1, NH + NKV), ALU.mult))
            dve.tensor_tensor(qk[:, i % 2, :], qk_c[:, :], qk_s[:, :], ALU.add).then_inc(sem("qk"), 1)
            dve.wait_ge(sem("st_hi"), NI * b + i + 1)
            q = qk[:, i % 2, 0:NH * HD].rearrange("p (h c) -> p h c", h=NH)
            k = qk[:, i % 2, NH * HD:QK].rearrange("p (h c) -> p h c", h=NKV)
            for c in (0, 2):
                own.did(dve.scalar_tensor_tensor(out=stq[:, :, c + 1, :], in0=q, scalar=HD ** -0.5, in1=stq[:, :, c, :], op0=ALU.mult, op1=ALU.subtract))
            for v in (0, 1):
                own.did(dve.tensor_tensor(stk[:, :, v, v, 2:4, :], bcast(k, 2, 2), stk[:, :, v, v, 0:2, :], ALU.subtract))
            vp = ps[:, base + 1, QK - 512:QKV - 512].rearrange("p (g c) -> p g c", g=NKV)
            own.link(dve.tensor_tensor(V[:, i, :, HD:2 * HD], vp, V[:, i, :, 0:HD], ALU.subtract))
            dve.sem_inc(sem("st_lo"), 1)
            for gi in (1, 3):
                dve.wait_ge(sem("str"), 4 * NI * b + 4 * i + gi + 1)
                dst = (qT if gi < 2 else kT)[:, 8:16, i * P:(i + 1) * P]
                dve.tensor_copy(dst, ps[:, 5, :].bitcast(F16).rearrange("p (a n) -> p a n", a=8)).then_inc(sem("ste_dve"), 1)

        def out_bank(dve, own, b, v):
            n = OG_END[v]
            i, q = n // NOG, n % NOG
            dve.wait_ge(sem("pv"), NU * b + v + 1)
            if q == 0 and i >= 2:
                dve.wait_ge(sem("atr"), NI * b + i - 1)
            O = ps[:, 4 + n % 2, :].rearrange("p (h c) -> p h c", h=OG)
            own.did(dve.tensor_reduce(osum[:, :, :], O[:, :, 0:2 * HD].rearrange("p h (t c) -> p h c t", t=2), AX, ALU.add))
            own.link(dve.reciprocal(rinv[:, :], O[:, :, 2 * HD]))
            dve.sem_inc(sem("o_read"), 1)
            own.link(dve.tensor_tensor(attn[:, i % 2, q * OG * HD:(q + 1) * OG * HD].rearrange("p (h c) -> p h c", h=OG), osum[:, :, :],
                                       bcast(rinv[:, :], 2, HD), ALU.mult))
            if q == NOG - 1:
                dve.sem_inc(sem("attn"), 1)

        def ffn_dve(dve, b, f, s, sg_, prod_):
            for j, (_, n) in enumerate(f.tiles):
                dve.wait_ge(sem(s + "_sg"), f.n * b + j + 1)
                if j >= 2:
                    dve.wait_ge(sem(s + "_hi"), f.n * b + j - 1)
                    dve.wait_ge(sem(s + "_lo"), f.n * b + j - 1)
                dve.scalar_tensor_tensor(out=prod_[0:n, j % 2, :], in0=ps[0:n, 2 + j % 2, :], scalar=1.0 / W_SCALE, in1=sg_[0:n, j % 2, :],
                                         op0=ALU.mult, op1=ALU.mult).then_inc(sem(s + "_prod"), 1)

        def ffn0_input_dve(dve, b, i):
            dve.wait_ge(sem("fxh"), NI * b + i + 1)
            dve.tensor_tensor(xl[:, :, i * P:(i + 1) * P], ps[:, 6, :].rearrange("p (k n) -> p k n", k=KD), xh[:, :, i * P:(i + 1) * P],
                              ALU.subtract).then_inc(sem("fxl"), 1)

        def round_dve(dve, own, b, f):
            if f is not None:
                own.link(dve.tensor_copy(x1r[:, :, :], x1[:, :, :]))
            if b is not None:
                for i in range(NI):
                    rope(dve, own, b, i)
            for u in range(UEND):
                if b is not None and 3 <= u <= NU + 2:
                    v = u - 3
                    i, w, h0, g = UNITS[v]
                    dve.wait_ge(sem("pth"), NU * b + v + 1)
                    if v >= 3:
                        dve.wait_ge(sem("pv"), NU * b + v - 2)
                    dve.tensor_tensor(ptl[:, v % 3, 0:g * w], ps[:, 2 + v % 2, 0:g * w], pth[:, v % 3, 0:g * w], ALU.subtract).then_inc(sem("ptl"), 1)
                if f is not None and u - 2 in U_AT:
                    n = U_AT[u - 2]
                    r = f0.tiles[n // 2][1]
                    dve.wait_ge(sem("f0_m"), NGU * f + n + 1)
                    if n >= 2:
                        dve.wait_ge(sem("f0_hi"), NGU * f + n - 1)
                        dve.wait_ge(sem("f0_lo"), NGU * f + n - 1)
                    dve.scalar_tensor_tensor(out=prod[0:r, n % 2, :], in0=ps[0:r, gu_bank(b, n), H2:S], scalar=0.5 / W_SCALE ** 2,
                                             in1=sg[0:r, n % 2, :], op0=ALU.mult, op1=ALU.mult).then_inc(sem("f0_prod"), 1)
                if b is not None and u < NU:
                    i, w, h0, g = UNITS[u]
                    dve.wait_ge(sem("score"), NU * b + u + 1)
                    if u >= 4:
                        dve.wait_ge(sem("exp"), NU * b + u - 3)
                    dve.tensor_reduce(nmax[:, u % 4, 0:g], ps[:, u % 2, 0:g * w].rearrange("p (g w) -> p g w", g=g), AX, ALU.max,
                                      negate=True).then_inc(sem("nmax"), 1)
                if f is not None and u - 1 in U_AT:
                    n = U_AT[u - 1]
                    r = f0.tiles[n // 2][1]
                    dve.wait_ge(sem("f0_sg"), NGU * f + n + 1)
                    dve.scalar_tensor_tensor(out=sg[0:r, n % 2, :], in0=sg[0:r, n % 2, :], scalar=1.0, in1=ps[0:r, gu_bank(b, n), 0:H2],
                                             op0=ALU.add, op1=ALU.mult).then_inc(sem("f0_m"), 1)
                if b is not None:
                    if u - 5 in OG_END:
                        out_bank(dve, own, b, u - 5)
                    for i in range(NI):
                        if u == LAST[i] + 11:
                            if i == 0:
                                dve.wait_ge(sem("w0_ready"), 1)
                            dve.wait_ge(sem("wo"), NI * b + i + 1)
                            own.link(dve.tensor_tensor(x1[:, i, :], ps[:, 6, :], xin[:, i, :], ALU.add))
                            dve.sem_inc(sem("x1_sum"), 1)
                            layer_norm_1(dve, own, x1[:, i, :], st6, mv[:, i % 2, :], ve[:, i % 2:i % 2 + 1], sem("ve1"))
                        if u == LAST[i] + 14:
                            dve.wait_ge(sem("rstd1"), NI * b + i + 1)
                            own.link(dve.tensor_scalar(x1[:, i, :], x1[:, i, :], mv[:, i % 2, 0:1], rstd[:, i % 2:i % 2 + 1], ALU.subtract, ALU.mult))
                            dve.sem_inc(sem("x1"), 1)
                    if u - 2 in FTR_AT:
                        ffn0_input_dve(dve, b, FTR_AT[u - 2])
                if f is not None:
                    if u - 1 in Y_AT:
                        i = Y_AT[u - 1]
                        dve.wait_ge(sem("y16"), NI * f + i + 1)
                        own.link(dve.tensor_tensor(x1r[:, i, :], y16[:, i % 2, :], x1r[:, i, :], ALU.add))
                        dve.sem_inc(sem("x2_sum"), 1)
                        layer_norm_1(dve, own, x1r[:, i, :], st6b, mvb[:, i % 2, :], veb[:, i % 2:i % 2 + 1], sem("ve2"))
                    if u - 3 in Y_AT:
                        i = Y_AT[u - 3]
                        dve.wait_ge(sem("rstd2"), NI * f + i + 1)
                        dve.tensor_scalar(x1r[:, i, :], x1r[:, i, :], mvb[:, i % 2, 0:1], rstdb[:, i % 2:i % 2 + 1], ALU.subtract,
                                          ALU.mult).then_inc(sem("x2_done"), 1)
            if b is not None:
                ffn0_input_dve(dve, b, NI - 1)
                if f is not None:
                    dve.wait_ge(sem("st_x2"), 16 * NI * (f + 1))

        def layer1_dve(dve, own):
            dve.wait_ge(sem("loop_act"), 1)
            dve.wait_ge(sem("loop_pe"), 1)
            dve.wait_ge(sem("loop_pool"), 1)
            dve.wait_ge(sem("ld_w1"), 16 * NLD1)
            own.link(dve.tensor_scalar(A8[:, :], A8[:, :], 80.0, None, ALU.min))
            dve.sem_inc(sem("alog"), 1)
            for k in range(2):
                own.did(dve.tensor_scalar(owT[:, k, :], owT[:, k, :], nw[:, k:k + 1], None, ALU.mult))
            dve.wait_ge(sem("c_exp"), 1)
            own.link(dve.tensor_scalar(al[:, 1:2], al[:, 1:2], 1.0, None, ALU.add))
            own.link(dve.reciprocal(al[:, 0:1], al[:, 1:2]))
            own.did(dve.tensor_scalar(al[:, 2:3], al[:, 0:1], -1.0, 1.0, ALU.mult, ALU.add))
            own.did(dve.tensor_scalar(al[:, 3:4], al[:, 0:1], 1.0, None, ALU.add))
            own.link(dve.tensor_scalar(A8[:, :], A8[:, :], -1.0, None, ALU.mult))
            dve.sem_inc(sem("c_small"), 1)
            for l in range(NB):
                dve.wait_ge(sem("xmid"), l + 1)
                dve.tensor_copy(uT[:, l, :], xmid[:, l, :]).then_inc(sem("u"), 1)
            for p in range(2):
                hydra_dve(dve, own, p)
            for l in range(NB):
                own.link(dve.tensor_scalar(uT[:, l, :], uT[:, l, :], al[:, 2:3], None, ALU.mult))
                own.link(dve.scalar_tensor_tensor(out=uT[:, l, :], in0=xmid[:, l, :], scalar=al[:, 3:4], in1=uT[:, l, :], op0=ALU.mult, op1=ALU.add))
                dve.sem_inc(sem("hT"), 1)
            for t in range(NT + 1):
                if t < NT:
                    dve.wait_ge(sem("up"), t + 1)
                    dve.wait_ge(sem(f"ld_x2r{t % 4}"), 16 * (t // 4 + 1))
                    own.link(dve.scalar_tensor_tensor(out=x3[:, t, :], in0=cscr[:, t % 4, :], scalar=2.0, in1=ps[:, t % 2, :], op0=ALU.mult, op1=ALU.add))
                    dve.sem_inc(sem("x3_sum"), 1)
                    own.link(dve.tensor_tensor(x3[:, t, :], x3[:, t, :], bup[:, :], ALU.add))
                    layer_norm_1(dve, own, x3[:, t, :], st6c, mvc[:, t % 2, :], vec[:, t % 2:t % 2 + 1], sem("ve3"))
                    dve.wait_ge(sem("rstd3"), t + 1)
                    own.link(dve.tensor_scalar(x3[:, t, :], x3[:, t, :], mvc[:, t % 2, 0:1], rstdc[:, t % 2:t % 2 + 1], ALU.subtract, ALU.mult))
                    dve.sem_inc(sem("x3"), 1)
                if t >= 1:
                    dve.wait_ge(sem("x3h"), t)
                    q = t - 1
                    dve.tensor_tensor(x3l[:, :, q * P:(q + 1) * P], ps[:, 4 + q % 2, :].rearrange("p (k n) -> p k n", k=KD),
                                      x3h[:, :, q * P:(q + 1) * P], ALU.subtract).then_inc(sem("x3l"), 1)
            with dve.Fori(0, NB) as b:
                own.enter(b, DVE_FFN1)
                ffn_dve(dve, b, f1, "f1", sg1, prod1)
                for i in range(NI):
                    dve.wait_ge(sem("f1_down"), NI * b + i + 1)
                    res = x3[:, bass.ds(NI * b + i, 1), :].rearrange("p o d -> p (o d)")
                    if i >= 2:
                        dve.wait_ge(sem(f"st_out{i % 2}"), 16 * (2 * b + i // 2))
                    own.link(dve.scalar_tensor_tensor(out=ob[:, i % 2, :], in0=ps[:, 4 + i % 2, :], scalar=1.0 / W_SCALE, in1=res,
                                                      op0=ALU.mult, op1=ALU.add))
                    dve.sem_inc(sem("ob_sum"), 1)
                    layer_norm_1(dve, own, ob[:, i % 2, :], st6c, mvc[:, i % 2, :], vec[:, i % 2:i % 2 + 1], sem("ve4"))
                    dve.wait_ge(sem("rstd4"), NI * b + i + 1)
                    own.link(dve.tensor_scalar(ob[:, i % 2, :], ob[:, i % 2, :], mvc[:, i % 2, 0:1], rstdc[:, i % 2:i % 2 + 1], ALU.subtract, ALU.mult))
                    dve.sem_inc(sem("out_ready"), 1)
                for r in range(2):
                    dve.wait_ge(sem(f"st_out{r}"), 16 * (2 * b + 2))
                own.leave(NB)

        def hydra_dve(dve, own, p):
            for st in range(NI):
                dve.wait_ge(sem("h_raw"), NI * p + st + 1)
                if st:
                    dve.wait_ge(sem("h_x"), NI * p + st)
                own.link(dve.tensor_tensor(yc, xraw[:, :, :], bcast(convw[:, 3, :], 1, NB), ALU.mult))
                own.link(dve.tensor_tensor(yc, yc, bcast(convb[:, :], 1, NB), ALU.add))
                dve.wait_ge(sem("h_taps"), NI * p + st + 1)
                for j in (1, 2, 3):
                    own.link(dve.tensor_tensor(yc[:, j:NB, :], yc[:, j:NB, :], conv_t[j], ALU.add))
                dve.sem_inc(sem("h_conv"), 1)
            fl = lambda a: a.rearrange("p a b -> p (a b)")
            v, e, mx, w, w2, q, dt, da = (sm[n][:, :, :] for n in ("v", "e", "mx", "w", "w2", "p", "dt", "da"))
            own.link(dve.tensor_tensor(v, dtr[:, :, :], bcast(dtb8[:, :], 1, NT), ALU.add))
            own.did(dve.tensor_scalar(mx, v, 0.0, None, ALU.max))
            own.link(dve.scalar_tensor_tensor(out=fl(e), in0=fl(v), scalar=-1.0, in1=fl(v), op0=ALU.mult, op1=ALU.max))
            dve.sem_inc(sem("h_v"), 1)
            for st in range(NI):
                dve.wait_ge(sem("h_x"), NI * p + st + 1)
                prod_cb = ty[:, 0, :].rearrange("p (l m n) -> p l m n", l=NB, m=NB)
                Cm = xc[:, st, :, DIN + DST:CONV]
                Bm = xc[:, st, :, DIN:DIN + DST]
                own.link(dve.tensor_tensor(prod_cb, bcast(Cm, 2, NB), bcast(Bm, 1, NB), ALU.mult))
                own.link(dve.tensor_reduce(CB[:, st, :], ty[:, 0, :].rearrange("p (a n) -> p a n", n=DST), AX, ALU.add))
            dve.wait_ge(sem("h_e"), p + 1)
            own.link(dve.tensor_scalar(w, e, 2.0, None, ALU.add))
            own.link(dve.reciprocal(w, w))
            own.link(dve.tensor_tensor(w, w, e, ALU.mult))
            own.link(dve.tensor_tensor(w2, w, w, ALU.mult))
            own.link(dve.tensor_scalar(q, w2, 1.0 / 17, None, ALU.mult))
            for odd in (15, 13, 11, 9, 7, 5, 3):
                own.link(dve.scalar_tensor_tensor(out=fl(q), in0=fl(q), scalar=1.0 / odd, in1=fl(w2), op0=ALU.add, op1=ALU.mult))
            own.link(dve.scalar_tensor_tensor(out=fl(q), in0=fl(q), scalar=1.0, in1=fl(w), op0=ALU.add, op1=ALU.mult))
            own.link(dve.scalar_tensor_tensor(out=fl(dt), in0=fl(q), scalar=2.0, in1=fl(mx), op0=ALU.mult, op1=ALU.add))
            own.link(dve.tensor_tensor(da, dt, bcast(A8[:, :], 1, NT), ALU.mult))
            dve.sem_inc(sem("h_adt"), 1)
            dv = sm["dt"][:, :, :].rearrange("p (s l) h -> p s l h", s=NI)
            av = sm["da"][:, :, :].rearrange("p (s l) h -> p s l h", s=NI)
            for m in range(3):
                own.did(dve.tensor_copy(Rf[:, :, m, m, :], dv[:, :, m, 0:NHY]))
                k = own.did(dve.tensor_copy(Sb[:, :, m, m, :], dv[:, :, m + 1, NHY:2 * NHY]))
            own.wait(k)
            dve.wait_ge(sem("h_da"), p + 1)
            own.did(dve.tensor_tensor(Rf[:, :, 1, 0:1, :], Rf[:, :, 0, 0:1, :], bcast(av[:, :, 1, 0:NHY], 2, 1), ALU.mult))
            own.link(dve.tensor_tensor(Sb[:, :, 1, 2:3, :], Sb[:, :, 2, 2:3, :], bcast(av[:, :, 2, NHY:2 * NHY], 2, 1), ALU.mult))
            own.did(dve.tensor_tensor(Rf[:, :, 2, 0:2, :], Rf[:, :, 1, 0:2, :], bcast(av[:, :, 2, 0:NHY], 2, 2), ALU.mult))
            own.link(dve.tensor_tensor(Sb[:, :, 0, 1:3, :], Sb[:, :, 1, 1:3, :], bcast(av[:, :, 1, NHY:2 * NHY], 2, 2), ALU.mult))
            for l in range(3):
                cf = CB[:, :, 4 * l:4 * l + l + 1]
                own.did(dve.tensor_tensor(M[:, :, l + 1, 0:l + 1, :], Rf[:, :, l, 0:l + 1, :], bcast(cf, 3, NHY), ALU.mult))
                cbk = CB[:, :, 4 * (l + 1) + l + 1:4 * (l + 1) + 4]
                own.did(dve.tensor_tensor(M[:, :, l, l + 1:4, :], Sb[:, :, l, l:3, :], bcast(cbk, 3, NHY), ALU.mult))
            marks = []
            for st in range(NI):
                for l in range(NB):
                    for h in range(NHY):
                        if len(marks) >= 3:
                            own.wait(marks[-3])
                        marks.append(own.did(dve.tensor_tensor_reduce(junk[:, len(marks) % 3, :], xc[:, st, l, 0:DIN], fcD[:, h, :], 1.0, 0.0,
                                                                      ALU.mult, ALU.add, Fd[:, st, l, h:h + 1])))
                own.wait(marks[-1])
                for l in range(NB):
                    k = own.did(dve.tensor_tensor(M[:, st, l, l, :], Fd[:, st, l, :], D4[:, :], ALU.add))
                own.wait(k)
                dve.sem_inc(sem("h_M"), 1)
                if st:
                    dve.wait_ge(sem("h_ytr"), NI * p + st)
                    dve.wait_ge(sem("h_ss"), NI * p + st)
                y4 = yy[:, :, :].rearrange("p l (h c) -> p l h c", h=NHY)
                t4 = ty[:, :, :].rearrange("p l (h c) -> p l h c", h=NHY)
                own.link(dve.tensor_tensor(y4, xs_b(st, 0), m_b(st, 0), ALU.mult))
                for m in (1, 2):
                    own.link(dve.tensor_tensor(t4, xs_b(st, m), m_b(st, m), ALU.mult))
                    own.link(dve.tensor_tensor(y4, y4, t4, ALU.add))
                dve.wait_ge(sem("h_yp"), NI * p + st + 1)
                own.link(dve.tensor_tensor(yy[:, :, :], yy[:, :, :], yp[:, :, :], ALU.add))
                own.link(dve.tensor_tensor(yy[:, :, :], yy[:, :, :], zg[:, st, :, :], ALU.mult))
                dve.sem_inc(sem("h_y"), 1)
                dve.wait_ge(sem("h_rs"), NI * p + st + 1)
                for l in range(NB):
                    k = own.did(dve.tensor_scalar(yy[:, l, :], yy[:, l, :], rs[:, st, l:l + 1], None, ALU.mult))
                own.wait(k)
                dve.sem_inc(sem("h_yn"), 1)
                dve.wait_ge(sem("h_out"), NI * p + st + 1)
                own.link(dve.tensor_copy(uT[:, :, st * P:(st + 1) * P], ps[:, 6, :].rearrange("p (l n) -> p l n", l=NB)))
                dve.sem_inc(sem("h_done"), 1)

        @block.vector
        def _(dve):
            own = Own(dve, sem("own_dve"))
            for n, k in enumerate("gud"):
                G, N8 = (KD, INTER0 // PACK) if k in "gu" else (f0.n, D // PACK)
                dve.wait_ge(sem("ld_zk"), 16 * (n + 1))
                z8 = zi[0:G, 0:N8 * PACK].rearrange("g (n j) -> g n j", j=PACK)
                for j in range(PACK):
                    m = own.did(dve.tensor_scalar(z8[:, :, j], zk[0:G, 0:N8], 4 * j, 15, ALU.logical_shift_right, ALU.bitwise_and))
                own.wait(m)
                dve.sem_inc(sem("zk_done"), 1)
                if n:
                    dve.wait_ge(sem("st_zs"), 16 * n)
                dve.tensor_scalar(zs[0:G, 0:N8 * PACK], zi[0:G, 0:N8 * PACK], W_SCALE, W_SCALE, ALU.mult, ALU.add).then_inc(sem("zs_done"), 1)
                dve.wait_ge(sem("zs_done"), n + 1)
            dve.wait_ge(sem("ld_shift"), 16)
            for c, (k, g, c0, n) in enumerate(CH0):
                r = rows0(k, g)
                dve.wait_ge(sem(f"ld_pk{c % 2}"), 48 * (c // 2 + 1))
                own.link(dve.tensor_scalar(nib[0:r, c % 2, 0:n], pk[0:r, c % 2, 0:n], shift[0:r, 0:1], 15, ALU.logical_shift_right, ALU.bitwise_and))
                dve.scalar_tensor_tensor(out=w0[k][0][0:r, g, c0:c0 + n], in0=nib[0:r, c % 2, 0:n], scalar=W_SCALE,
                                         in1=zb[0:r, c % 2, 0:n], op0=ALU.mult, op1=ALU.subtract).then_inc(sem("deq_d"), 1)
            dve.wait_ge(sem("ld_wa"), 64)
            dve.wait_ge(sem("consts"), 1)
            round_dve(dve, own, 0, None)
            with dve.Fori(0, NB - 1) as f:
                own.enter(f, DVE_LOOP)
                round_dve(dve, own, f + 1, f)
                own.leave(NB - 1)
            round_dve(dve, own, None, NB - 1)
            dve.sem_inc(sem("loop_dve"), 1)
            layer1_dve(dve, own)

        def stage_transposes(pe, b, i):
            pe.wait_ge(sem("st_lo"), NI * b + i + 1)
            for gi in range(4):
                n = 4 * i + gi
                if gi % 2 == 0 and n >= 2:
                    pe.wait_ge(sem("ste_act"), 2 * NI * b + n // 2)
                if gi % 2 == 1 and n >= 2:
                    pe.wait_ge(sem("ste_dve"), 2 * NI * b + n // 2)
                dst = ps[:, 4 + gi % 2, :].bitcast(F16)
                for a in range(8):
                    if gi < 2:
                        src = stq[:, 2 * (8 * gi + a):2 * (8 * gi + a) + 2, :, :].rearrange("p h c d -> p (h c d)")
                    else:
                        g, var = divmod(8 * (gi - 2) + a, 2)
                        src = stk[:, g, var, :, :, :].rearrange("p e c d -> p (e c d)")
                    ins = pe.transpose(dst[:, a * P:(a + 1) * P], src, identh[:, :])
                ins.then_inc(sem("str"), 1)

        def ffn_pe(pe, b, f, s, w, x_at, inter):
            for j, (c0, n) in enumerate(f.tiles):
                if j >= 2:
                    pe.wait_ge(sem(s + "_sg"), f.n * b + j - 1)
                    pe.wait_ge(sem(s + "_prod"), f.n * b + j - 1)
                for m, bank in (("g", j % 2), ("u", 2 + j % 2)):
                    last = 3 * KD - 1
                    at = 0
                    for k in range(KD):
                        for pw, px in ((0, 0), (0, 1), (1, 0)):
                            ins = pe.matmul(ps[0:n, bank, :], w[m][pw][:, k, c0:c0 + n], x_at(px, k), start=(at == 0), stop=(at == last))
                            at += 1
                ins.then_inc(sem(s + "_gu"), 1)
            pe.wait_ge(sem(s + "_lo"), f.n * (b + 1))
            for i in range(NI):
                if i >= 2:
                    pe.wait_ge(sem("y16" if s == "f0" else "ob_sum"), NI * b + i - 1)
                at = 0
                for j, (_, n) in enumerate(f.tiles):
                    for pi, pw in ((0, 0), (0, 1), (1, 0)):
                        ins = pe.matmul(ps[:, 4 + i % 2, :], inter[pi][0:n, j, i * P:(i + 1) * P], w["d"][pw][0:n, j, :],
                                        start=(at == 0), stop=(at == 3 * f.n - 1))
                        at += 1
                ins.then_inc(sem(s + "_down"), 1)

        def projections_pe(pe, b, f):
            pe.wait_ge(sem("ld_x"), 16 * (b + 1))

            def xtr(i):
                for k in range(KD):
                    ins = pe.transpose(ps[:, 6 + i % 2, k * P:(k + 1) * P], xin[:, i, k * P:(k + 1) * P], identf[:, :])
                ins.then_inc(sem("xtr"), 1)

            if f is not None:
                pe.wait_ge(sem("fxl"), NI * b)
            xtr(0)
            xtr(1)
            for i in range(NI):
                pe.wait_ge(sem("xte"), NI * b + i + 1)
                if i >= 2:
                    pe.wait_ge(sem("st_lo"), NI * b + i - 1)
                for k in range(KD):
                    pe.matmul(ps[:, 2 * (i % 2), :], xT[:, i % 2, k, :], wqkv[:, k, 0:512], start=(k == 0), stop=(k == KD - 1))
                for k in range(KD):
                    ins = pe.matmul(ps[:, 2 * (i % 2) + 1, 0:QKV - 512], xT[:, i % 2, k, :], wqkv[:, k, 512:QKV], start=(k == 0), stop=(k == KD - 1))
                ins.then_inc(sem("proj"), 1)
                if i + 2 < NI:
                    xtr(i + 2)
                if i >= 1:
                    stage_transposes(pe, b, i - 1)
            stage_transposes(pe, b, NI - 1)
            pe.wait_ge(sem("ste_act"), 2 * NI * (b + 1))
            pe.wait_ge(sem("ste_dve"), 2 * NI * (b + 1))

        def ffn0_input_pe(pe, b, i):
            pe.wait_ge(sem("x1"), NI * b + i + 1)
            pe.wait_ge(sem("x1_sum"), NI * b + max(i, NI - 2) + 1)
            if i:
                pe.wait_ge(sem("fxl"), NI * b + i)
            for k in range(KD):
                ins = pe.transpose(ps[:, 6, k * P:(k + 1) * P], x1[:, i, k * P:(k + 1) * P], identf[:, :])
            ins.then_inc(sem("ftr"), 1)

        def ffn0_gate_up_pe(pe, b, f, n, m):
            j, half = divmod(n, 2)
            c0, r = f0.tiles[j]
            cols = slice(0, H2) if m == "g" else slice(H2, S)
            if m == "g":
                before = GU_PREV[n] if b is not None else (n - 2 if n >= 2 else None)
                if before is not None:
                    pe.wait_ge(sem("f0_prod"), NGU * f + before + 1)
                if b is not None and GU_BANK[n] == 6:
                    done = sum(hi < G_SLOT[n] for lo, hi in OUT6)
                    if done:
                        pe.wait_ge(sem("x1_sum"), NI * b + done)
            at = 0
            for k in range(KD):
                for pw, px in ((0, xh), (0, xl), (1, xh)):
                    ins = pe.matmul(ps[0:r, gu_bank(b, n), cols], w0[m][pw][:, k, c0:c0 + r], px[:, k, half * H2:half * H2 + H2],
                                    start=(at == 0), stop=(at == 3 * KD - 1))
                    at += 1
            if m == "u":
                ins.then_inc(sem("f0_gu"), 1)

        def ffn0_down_pe(pe, b, f, i, piece):
            ahead = 1 if b is not None else 2
            if piece == 0:
                if i == 0:
                    pe.wait_ge(sem("f0_lo"), NGU * (f + 1))
                    pe.wait_ge(sem("f0_prod"), NGU * (f + 1))
                if i >= ahead:
                    pe.wait_ge(sem("y16"), NI * f + i - ahead + 1)
            steps = [(j, r, pi, pw) for j, (_, r) in enumerate(f0.tiles) for pi, pw in ((0, 0), (0, 1), (1, 0))]
            each = -(-len(steps) // DP)
            for at in range(piece * each, min(len(steps), piece * each + each)):
                j, r, pi, pw = steps[at]
                ins = pe.matmul(ps[:, down_bank(b, i), :], int0[pi][0:r, j, i * P:(i + 1) * P], w0["d"][pw][0:r, j, :],
                                start=(at == 0), stop=(at == len(steps) - 1))
            if piece == DP - 1:
                ins.then_inc(sem("f0_down"), 1)

        def round_pe(pe, b, f):
            if b is not None:
                if f is not None:
                    pe.wait_ge(sem("stk_zero"), f + 1)
                projections_pe(pe, b, f)
            else:
                pe.wait_ge(sem("fxl"), NI * NB)
            for u in range(UEND):
                if b is not None:
                    if u < NU:
                        i, w, h0, g = UNITS[u]
                        if u >= 2:
                            pe.wait_ge(sem("exp"), NU * b + u - 1)
                        for x in range(g):
                            h = h0 + x
                            pe.matmul(ps[:, u % 2, x * w:(x + 1) * w], qT[:, h // 2, i * P:(i + 1) * P], kT[:, 2 * (h // NREP) + h % 2, 0:w],
                                      start=True, stop=False)
                            ins = pe.matmul(ps[:, u % 2, (x + 1) * w - P:(x + 1) * w], identb[:, :], mask[:, :], start=False, stop=True)
                        ins.then_inc(sem("score"), 1)
                    if 2 <= u <= NU + 1:
                        v = u - 2
                        i, w, h0, g = UNITS[v]
                        pe.wait_ge(sem("exp"), NU * b + v + 1)
                        if v >= 2:
                            pe.wait_ge(sem("ptl"), NU * b + v - 1)
                        for c in range(0, g * w, P):
                            ins = pe.transpose(ps[:, 2 + v % 2, c:c + P], Pe[:, v % 2, c:c + P], identf[:, :])
                        ins.then_inc(sem("ptr"), 1)
                    if 4 <= u <= NU + 3:
                        v = u - 4
                        i, w, h0, g = UNITS[v]
                        pe.wait_ge(sem("ptl"), NU * b + v + 1)
                        n = i * NOG + h0 // OG
                        if h0 % OG == 0 and n >= 2:
                            pe.wait_ge(sem("o_read"), NI * NOG * b + n - 1)
                        for x in range(g):
                            h = h0 + x
                            dst = ps[:, 4 + n % 2, (h % OG) * 64:(h % OG) * 64 + VW]
                            for part, src in ((0, pth), (1, ptl)):
                                for j in range(i + 1):
                                    c = x * w + j * P
                                    ins = pe.matmul(dst, src[:, v % 3, c:c + P], V[:, j, h // NREP, :],
                                                    start=(part == 0 and j == 0), stop=(part == 1 and j == i))
                        ins.then_inc(sem("pv"), 1)
                    for i in range(NI):
                        if u == LAST[i] + 7:
                            pe.wait_ge(sem("attn"), NI * b + i + 1)
                            if f is not None:
                                pe.wait_ge(sem("f0_prod"), NGU * f + 1 + max(n for n in range(NGU) if GU_BANK[n] == 6 and G_SLOT[n] < u))
                            if i == NI - 1:
                                pe.wait_ge(sem("fxl"), NI * b + i)
                            elif i:
                                pe.wait_ge(sem("x1_sum"), NI * b + i)
                            for k in range(KD):
                                ins = pe.transpose(ps[:, 6, k * P:(k + 1) * P], attn[:, i % 2, k * P:(k + 1) * P], identf[:, :])
                            ins.then_inc(sem("atr"), 1)
                        if u == LAST[i] + 9:
                            pe.wait_ge(sem("ate"), NI * b + i + 1)
                            for k in range(KD):
                                ins = pe.matmul(ps[:, 6, :], aT[:, k, :], wo[:, k, :], start=(k == 0), stop=(k == KD - 1))
                            ins.then_inc(sem("wo"), 1)
                    if u in FTR_AT:
                        ffn0_input_pe(pe, b, FTR_AT[u])
                if f is not None:
                    if u in G_AT:
                        ffn0_gate_up_pe(pe, b, f, G_AT[u], "g")
                    if u in U_AT:
                        ffn0_gate_up_pe(pe, b, f, U_AT[u], "u")
                    if u in DOWN_AT:
                        ffn0_down_pe(pe, b, f, *DOWN_AT[u])
            if b is not None:
                ffn0_input_pe(pe, b, NI - 1)

        def layer1_pe(pe):
            pe.wait_ge(sem("ld_w1"), 16 * NLD1)
            pe.wait_ge(sem("loop_act"), 1)
            pe.wait_ge(sem("loop_dve"), 1)
            for l in range(NB):
                pe.wait_ge(sem("ld_x2"), 16 * (l + 1))
                for i in range(NI):
                    if l:
                        pe.wait_ge(sem("c1_te"), NI * (l - 1) + i + 1)
                    for k in range(KD):
                        ins = pe.transpose(ps[:, i, k * P:(k + 1) * P], x2a[:, i, k * P:(k + 1) * P], identf[:, :])
                    ins.then_inc(sem("c1_tr"), 1)
                pe.wait_ge(sem("c1_te"), NI * (l + 1))
                if l >= 2:
                    pe.wait_ge(sem("xmid"), l - 1)
                for k in range(KD):
                    ins = pe.matmul(ps[:, 4 + l % 2, :], wdT[:, k, :], xTb[:, k, :], start=(k == 0), stop=(k == KD - 1))
                ins.then_inc(sem("c1_dn"), 1)
            pe.wait_ge(sem("u"), NB)
            pe.wait_ge(sem("c_small"), 1)
            for p in range(2):
                for st in range(NI):
                    if st or p:
                        pe.wait_ge(sem("h_raw"), NI * p + st)
                    for l in range(NB):
                        lhs = uT[:, l, st * P:(st + 1) * P]
                        pe.matmul(ps[:, l, :], lhs, inwT[:, 0:512], start=True, stop=True)
                        ins = pe.matmul(ps[:, 4 + st % 2, l * 64:l * 64 + PROJ - 512], lhs, inwT[:, 512:PROJ], start=True, stop=True)
                    ins.then_inc(sem("h_in"), 1)
                for st in range(NI):
                    pe.wait_ge(sem("h_yn"), NI * p + st + 1)
                    if st:
                        pe.wait_ge(sem("h_yT"), NI * p + st)
                    for k in range(2):
                        for l in range(NB):
                            ins = pe.transpose(ps[:, 4 + k, l * P:(l + 1) * P], yy[:, l, k * P:(k + 1) * P], identf[:, :])
                    ins.then_inc(sem("h_ytr"), 1)
                    pe.wait_ge(sem("h_yT"), NI * p + st + 1)
                    if st:
                        pe.wait_ge(sem("h_done"), NI * p + st)
                    for k in range(2):
                        ins = pe.matmul(ps[:, 6, :], owT[:, k, :], yT[:, k, :], start=(k == 0), stop=(k == 1))
                    ins.then_inc(sem("h_out"), 1)
                pe.wait_ge(sem("h_done"), NI * (p + 1))
            for t in range(NT + 1):
                if t < NT:
                    l, st = divmod(t, NI)
                    pe.wait_ge(sem("hT"), l + 1)
                    if t >= 2:
                        pe.wait_ge(sem("x3_sum"), t - 1)
                    pe.matmul(ps[:, t % 2, :], uT[:, l, st * P:(st + 1) * P], wuT[:, :], start=True, stop=True).then_inc(sem("up"), 1)
                if t >= 1:
                    q = t - 1
                    pe.wait_ge(sem("x3"), q + 1)
                    if q >= 2:
                        pe.wait_ge(sem("x3l"), q - 1)
                    for k in range(KD):
                        ins = pe.transpose(ps[:, 4 + q % 2, k * P:(k + 1) * P], x3[:, q, k * P:(k + 1) * P], identf[:, :])
                    ins.then_inc(sem("x3tr"), 1)
            pe.wait_ge(sem("x3l"), NT)
            pe.wait_ge(sem("ld_wf"), 16 * 6)
            with pe.Fori(0, NB) as b:
                ffn_pe(pe, b, f1, "f1", w1, lambda part, k: (x3h, x3l)[part][:, k, bass.ds(b * S, S)], int1)

        @block.tensor
        def _(pe):
            pe.wait_ge(sem("consts"), 1)
            pe.wait_ge(sem("ld_wa"), 64)
            round_pe(pe, 0, None)
            pe.wait_ge(sem("w0_ready"), 1)
            with pe.Fori(0, NB - 1) as f:
                round_pe(pe, f + 1, f)
            round_pe(pe, None, NB - 1)
            pe.sem_inc(sem("loop_pe"), 1)
            layer1_pe(pe)


def rope_tables():
    inv = (1.0 / 10000.0 ** (np.arange(0, HD, 2, dtype=np.float32) / HD)).astype(np.float32)
    f = np.arange(S, dtype=np.float32)[:, None] * inv[None, :]
    c, s = np.cos(f), np.sin(f)
    return np.repeat(c, 2, axis=1), np.stack([-s, s], axis=-1).reshape(S, HD)


def kernel(**inputs):
    import concourse.bacc as _bacc
    from concourse.bass_utils import run_bass_kernel_spmd as _run

    a = {k: np.asarray(v) for k, v in inputs.items()}
    cos, sin = rope_tables()
    data = {
        "x": a["L0_attn_hidden_states"],
        "wqkvT": np.concatenate([a["L0_attn_Wq"].T, a["L0_attn_Wk"].T, a["L0_attn_Wv"].T], axis=1),
        "woT": a["L0_attn_Wo"].T,
        "cos": cos, "sin": sin,
        "shift": (np.arange(P, dtype=np.int32) % PACK * 4).reshape(P, 1),
        "inwT": a["L1_attn_hy_in_w"].T, "owT": a["L1_attn_hy_out_w"].T, "wdT": a["L1_attn_w_down"].T, "wuT": a["L1_attn_w_up"].T,
        "bup": a["L1_attn_b_up"], "bdn": a["L1_attn_b_down"],
        "convw": a["L1_attn_hy_conv_w"][:, 0, -NB:].T, "convb": a["L1_attn_hy_conv_b"],
        "fcD": a["L1_attn_hy_fcD_w"], "Alog": a["L1_attn_hy_A_log"], "dtb": a["L1_attn_hy_dt_bias"], "D": a["L1_attn_hy_D"],
        "nw": a["L1_attn_hy_norm_w"].reshape(2, P).T, "gate": a["L1_attn_gate1"].reshape(1),
    }
    for k, name in (("g", "gate"), ("u", "up"), ("d", "down")):
        data[f"q0{k}"] = a[f"L0_ffn_{name}_qweight"]
        data[f"s0{k}"] = a[f"L0_ffn_{name}_scales"]
        data[f"z0{k}"] = a[f"L0_ffn_{name}_zeros"]
        data[f"q1{k}"] = a[f"L1_ffn_{name}_w"]
        data[f"s1{k}"] = a[f"L1_ffn_{name}_s"]
        data[f"z1{k}"] = a[f"L1_ffn_{name}_z"]
    data = {f"in_{k}": np.ascontiguousarray(v) for k, v in data.items()}
    nc = _bacc.Bacc("TRN2", target_bir_lowering=False, num_devices=1)
    A = {k[3:]: nc.dram_tensor(k, v.shape, mybir.dt.from_np(v.dtype), kind="ExternalInput").ap() for k, v in data.items()}
    A["out"] = nc.dram_tensor("out", (NB, S, D), F32, kind="ExternalOutput").ap()
    build(nc, A)
    return _run(nc, [data], core_ids=[0]).results[0]["out"]
```

```python
from contextlib import ExitStack

import numpy as np
import concourse.bass as bass
from concourse import mybir

F32 = mybir.dt.float32
F16 = mybir.dt.float16
BF16 = mybir.dt.bfloat16
I32 = mybir.dt.int32
ACT = mybir.ActivationFunctionType
ALU = mybir.AluOpType
AX = mybir.AxisListType.X

P = 128
NB, S, D = 4, 512, 512
NI = S // P
NT = NB * NI
KD = D // P
NH, NKV, HD = 32, 8, 16
NREP = NH // NKV
QKV = (NH + 2 * NKV) * HD
QK = (NH + NKV) * HD
VW = 34
W_SCALE = 256.0
INTER0, INTER1 = 1376, 1792
PACK = 8
DM, DIN, DST, NHY = 128, 256, 16, 4
CONV = DIN + 2 * DST
PROJ = 2 * DIN + 2 * DST + 2 * NHY
MASKED = -1e30
EPS = 1e-5


def bcast(ap, axis, n):
    shape = list(ap.shape)
    shape.insert(axis, n)
    return ap.unsqueeze(axis).broadcast_to(shape)


class Own:

    def __init__(self, eng, sem):
        self.eng, self.sem, self.base, self.n = eng, sem, 0, 0

    def did(self, ins):
        ins.then_inc(self.sem, 1)
        self.n += 1
        return self.base + self.n

    def wait(self, mark):
        self.eng.wait_ge(self.sem, mark)

    def link(self, ins):
        self.wait(self.did(ins))

    def enter(self, i, per):
        self.start, self.per = self.base + self.n, per
        self.base, self.n = self.start + i * per, 0

    def leave(self, times):
        assert self.n == self.per, f"steps of the loop's body: {self.n}, not {self.per}"
        self.base, self.n = self.start + times * self.per, 0


class Ffn:

    def __init__(self, inter):
        self.inter = inter
        self.tiles = [(f * P, min(P, inter - f * P)) for f in range(-(-inter // P))]
        self.n = len(self.tiles)


def units_of_batch():
    out = []
    for i in range(NI):
        w = (i + 1) * P
        g = 512 // w
        out += [(i, w, h, g) for h in range(0, NH, g)]
    return out


NLD1 = 14
DVE_LOOP = 109
POOL_LOOP = 48
DVE_LOOP1 = 183


UNITS = units_of_batch()
NU = len(UNITS)
OG = 8
NOG = NH // OG
LAST = {i: max(n for n, u in enumerate(UNITS) if u[0] == i) for i in range(NI)}
OG_END = {}
for _n, (_i, _w, _h, _g) in enumerate(UNITS):
    if (_h + _g) % OG == 0:
        OG_END[_n] = _i * NOG + (_h + _g) // OG - 1


F0 = Ffn(INTER0)
NGU = 2 * F0.n
H2 = S // 2
G_AT = {1 + 2 * n * 4 // 3: n for n in range(NGU)}
U_AT = {1 + (2 * n + 1) * 4 // 3: n for n in range(NGU)}
OUT6 = [(LAST[i] + 7, LAST[i] + 11) for i in range(NI)]
G_SLOT = {n: u for u, n in G_AT.items()}
GU_BANK = {}
for _u, _n in sorted(G_AT.items()):
    _busy = any(lo - 2 <= _u <= hi for lo, hi in OUT6)
    GU_BANK[_n] = 7 if _busy or GU_BANK.get(_n - 1) == 6 else 6
GU_PREV = {n: max([m for m in range(n) if GU_BANK[m] == GU_BANK[n]], default=None) for n in range(NGU)}
DOWN0 = max(U_AT) + 3
DP = 5
DOWN_AT = {DOWN0 + (DP + 1) * i + k: (i, k) for i in range(NI) for k in range(DP)}
Y_AT = {DOWN0 + (DP + 1) * i + DP: i for i in range(NI)}
FTR_AT = {DOWN0 + 8 + 5 * i: i for i in range(NI - 1)}
UEND = NU + 17
W1C = 448
CHG = [(k, c) for k in "gu" for c in range(0, INTER1, W1C)]
ND1 = 4
NC1R = len(CHG) + ND1
W1_AT = {1 + 8 * c: c for c in range(NC1R)}
HW = INTER0 // 2
CH0 = [(k, g, c, HW) for k in "gu" for g in range(KD) for c in (0, HW)] + [("d", g, 0, D) for g in range(F0.n)]
CH0_AT = {1 + 2 * c: c for c in range(len(CH0))}


F1 = Ffn(INTER1)
NG1 = 2 * F1.n
PASS_AT = (0, 16)
MIX = 32
HEAD = MIX + 6
GU1 = [PASS_AT[0] + k for k in range(1, 15)] + [PASS_AT[1] + k for k in range(1, 15)]
GU1_AT = {u: n for n, u in enumerate(GU1)}
assert len(GU1) == NG1
DP1 = 2
DOWN1 = max(GU1) + 2
DOWN1_AT = {DOWN1 + DP1 * i + k: (i, k) for i in range(NB) for k in range(DP1)}
OUT1_AT = {DOWN1 + DP1 * (i + 1): i for i in range(NB)}
UEND1 = DOWN1 + DP1 * (NB + 1) + 1


def build(nc, A):
    ctx = ExitStack()
    sems = {}

    def sem(name):
        if name not in sems:
            sems[name] = ctx.enter_context(nc.semaphore(name))
        return sems[name]

    def allocator(stack):
        return lambda name, shape, dt=F32: stack.enter_context(nc.sbuf_tensor(name, shape, dt))

    f0, f1 = Ffn(INTER0), Ffn(INTER1)
    with ctx:
        sb = allocator(ctx)
        ps = ctx.enter_context(nc.psum_tensor("ps", [P, 8, 512], F32))
        identf = sb("identf", [P, P])
        identh = sb("identh", [P, P], F16)
        identb = sb("identb", [P, P], BF16)
        mask = sb("mask", [P, P], BF16)
        neghalf = sb("neghalf", [P, 4])

        L = ExitStack()
        lb = allocator(L)
        w0 = {k: [lb(f"w0{k}{p}", [P, KD, INTER0] if k in "gu" else [P, f0.n, D], F16) for p in "hl"] for k in "gud"}
        shift = lb("shift", [P, 1], I32)
        costab = lb("costab", [P, NI, HD])
        sintab = lb("sintab", [P, NI, HD])
        wqkv = lb("wqkv", [P, KD, QKV])
        wo = lb("wo", [P, KD, D])
        xin = lb("xin", [P, NI, D])
        V = lb("V", [P, NI, NKV, VW], F16)
        Pe = lb("Pe", [P, 2, 512])
        pth = lb("pth", [P, 3, 512], F16)
        ptl = lb("ptl", [P, 3, 512], F16)
        nmax = lb("nmax", [P, 4, 4])
        osum = lb("osum", [P, OG, HD])
        rinv = lb("rinv", [P, OG])
        attn = lb("attn", [P, 2, D])
        aT = lb("aT", [P, KD, P])
        st6 = lb("st6", [P, 6])
        mv = lb("mv", [P, 2, 2])
        ve = lb("ve", [P, 2])
        rstd = lb("rstd", [P, 2])
        st6b = lb("st6b", [P, 6])
        mvb = lb("mvb", [P, 2, 2])
        veb = lb("veb", [P, 2])
        rstdb = lb("rstdb", [P, 2])
        qT = lb("qT", [P, NH // 2, S], F16)
        kT = lb("kT", [P, NKV * 2, S], F16)
        LI = ExitStack()
        li = allocator(LI)
        int0 = [li(f"int0{p}", [P, f0.n, S], F16) for p in "hl"]
        LI.close()
        xT = lb("xT", [P, 2, KD, P])
        qk_c = lb("qk_c", [P, QK])
        qk_s = lb("qk_s", [P, QK])
        qk = lb("qk", [P, 2, QK])
        stq = lb("stq", [P, NH, 4, HD], F16)
        stk = lb("stk", [P, NKV, 2, 2, 4, HD], F16)
        LS = ExitStack()
        ls = allocator(LS)
        wv = ls("wv", [P, HW])
        pk = ls("pk", [P, 2, HW], I32)
        zb = ls("zb", [P, 2, HW], F16)
        nib = ls("nib", [P, 2, HW], I32)
        zk = ls("zk", [16, 172], I32)
        zi = ls("zi", [16, INTER0], I32)
        zs = ls("zs", [16, INTER0], F16)
        LS.close()
        x1r = lb("x1r", [P, NI, D])
        sg = lb("sg", [P, 2, H2])
        prod = lb("prod", [P, 2, H2])
        y16 = lb("y16", [P, 2, D], F16)
        vq = lb("vq", [P, 512])
        vz = lb("vz", [P, 512], I32)
        vs = lb("vs", [P, 512])
        vh = lb("vh", [P, 512], F16)
        vl = lb("vl", [P, 512], F16)
        x1 = lb("x1", [P, NI, D])
        xh = lb("xh", [P, KD, S], F16)
        xl = lb("xl", [P, KD, S], F16)
        L.close()

        C = ExitStack()
        cb = allocator(C)
        w1 = {k: [cb(f"w1{k}{p}", [P, KD, INTER1] if k in "gu" else [P, f1.n, D], F16) for p in "hl"] for k in "gud"}
        x3 = cb("x3", [P, NB, D])
        x3r = cb("x3r", [P, NB, D])
        x3h = cb("x3h", [P, KD, S], F16)
        x3l = cb("x3l", [P, KD, S], F16)
        int1 = [cb(f"int1{p}", [P, f1.n, S], F16) for p in "hl"]
        sg1 = cb("sg1", [P, 2, H2])
        prod1 = cb("prod1", [P, 2, H2])
        x2a = cb("x2a", [P, NB, D])
        CX = ExitStack()
        cx = allocator(CX)
        xTb = cx("xTb", [P, KD, S])
        CX.close()
        xraw = cb("xraw", [P, NB, CONV])
        yc = cb("yc", [P, NB, CONV])
        xc = cb("xc", [P, NB, CONV])
        zg = cb("zg", [P, NB, DIN])
        yy = cb("yy", [P, NB, DIN])
        ty = cb("ty", [P, NB, DIN])
        yp = cb("yp", [P, NB, DIN])
        uT = cb("uT", [P, S])
        xmid = cb("xmid", [P, S])
        inwT = cb("inwT", [P, PROJ])
        owT = cb("owT", [P, 2, DM])
        wdT = cb("wdT", [P, KD, DM])
        wuT = cb("wuT", [P, D])
        bup = cb("bup", [P, D])
        convw = cb("convw", [P, NB, CONV])
        convb = cb("convb", [P, CONV])
        fcD = cb("fcD", [P, NHY, DIN])
        dtr = cb("dtr", [P, NB, 2 * NHY])
        sm = {n: cb(f"sm_{n}", [P, NB, 2 * NHY]) for n in ("v", "e", "mx", "w", "w2", "p", "dt", "da")}
        CB = cb("CB", [P, 16])
        Rf = cb("Rf", [P, 3, 3, NHY])
        Sb = cb("Sb", [P, 3, 3, NHY])
        M = cb("M", [P, NB, NB, NHY])
        Fd = cb("Fd", [P, NB, NHY])
        ss = cb("ss", [P, NB])
        rs = cb("rs", [P, NB])
        A8 = cb("A8", [P, 2 * NHY])
        dtb8 = cb("dtb8", [P, 2 * NHY])
        D4 = cb("D4", [P, NHY])
        nw = cb("nw", [P, 2])
        bdn = cb("bdn", [P, 1])
        al = cb("al", [P, 4])
        st6c = cb("st6c", [P, 6])
        mvc = cb("mvc", [P, NB, 2])
        vec = cb("vec", [P, NB])
        rstdc = cb("rstdc", [P, NB])
        st6d = cb("st6d", [P, 6])
        mvd = cb("mvd", [P, 2, 2])
        ved = cb("ved", [P, 2])
        rstdd = cb("rstdd", [P, 2])
        C.close()

        zs_dram = {k: nc.dram_tensor(f"zs_{k}", [16, INTER0], F16, kind="Internal").ap() for k in "gud"}
        x2_dram = nc.dram_tensor("x2_dram", [NT, P, D], F32, kind="Internal").ap()
        w1_dram = {k: [nc.dram_tensor(f"w1_{k}{p}", [KD, P, INTER1] if k in "gu" else [f1.n, P, D], F16, kind="Internal").ap() for p in "hl"]
                   for k in "gud"}
        w1_rows = {k: A[f"q1{k}"].rearrange("(g p) n -> g p n", p=P) for k in "gud"}

        x2_blocks = x2_dram.rearrange("(l i) p d -> i p l d", l=NB)
        out_tiles = A["out"].rearrange("b (i p) d -> b i p d", p=P)
        x_rows = A["x"].rearrange("b (i p) d -> b p i d", p=P)
        block = ctx.enter_context(nc.Block())
        def w1_chunk(f, c):
            last = isinstance(f, int) and f == NB - 1
            if c < len(CHG):
                k, c0 = CHG[c]
                return k, 0 if last else f + 1, slice(c0, c0 + W1C), W1C
            return "d", ND1 * f + c - len(CHG), slice(0, D), D

        def one(ap, g, cols):
            return ap[bass.ds(g, 1), :, cols].rearrange("o p n -> (o p) n")

        NC1L = len(CHG) + f1.n - ND1 * (NB - 1)
        NC1 = NC1R * (NB - 1) + NC1L

        def gu_bank(b, n):
            return GU_BANK[n] if b is not None else 6 + n % 2

        def down_bank(b, i):
            return 7 if b is not None else 6 + i % 2

        def rows0(k, g):
            return min(P, INTER0 - g * P) if k == "d" else P

        t1 = yy[:, :, :].rearrange("p a b -> p (a b)")[:, 0:3 * CONV].rearrange("p (l c) -> p l c", l=3)
        t2 = ty[:, :, :].rearrange("p a b -> p (a b)")[:, 0:2 * CONV].rearrange("p (l c) -> p l c", l=2)
        t3 = yp[:, :, :].rearrange("p a b -> p (a b)")[:, 0:CONV].rearrange("p (l c) -> p l c", l=1)
        conv_t = {1: t1, 2: t2, 3: t3}
        yT = ty[:, :, :].rearrange("p a b -> p (a b)").rearrange("p (k n) -> p k n", k=2)
        yq = xraw[:, :, :].rearrange("p a b -> p (a b)")[:, 0:NB * DIN].rearrange("p (a b) -> p a b", a=NB)
        junk = xraw[:, :, :].rearrange("p a b -> p (a b)")[:, 0:3 * DIN].rearrange("p (a b) -> p a b", a=3)

        def xs_b(m):
            return bcast(xc[:, m, 0:DIN].rearrange("p (h c) -> p h c", h=NHY), 1, NB)

        def m_b(m):
            return bcast(M[:, :, m, :], 3, DIN // NHY)

        def w1_load(sp, c, k, g, cols, n):
            sp.wait_ge(sem("w1_lo"), c)
            sp.sem_inc(sem("sp_seen"), 1)
            sp.dma_start(vq[:, 0:n].bitcast(I32), one(w1_rows[k], g, cols)).then_inc(sem("ld_w1c"), 16)
            sp.dma_start(vz[:, 0:n], A[f"z1{k}"][bass.ds(g, 1), cols].rearrange("o n -> (o n)").partition_broadcast(P)).then_inc(sem("ld_w1c"), 16)
            sp.dma_start(vs[:, 0:n], A[f"s1{k}"][bass.ds(g, 1), cols].rearrange("o n -> (o n)").partition_broadcast(P)).then_inc(sem("ld_w1c"), 16)

        def w1_store(sp, c, k, g, cols, n):
            sp.wait_ge(sem("w1_lo"), c + 1)
            sp.sem_inc(sem("sp_seen"), 1)
            sp.dma_start(one(w1_dram[k][0], g, cols), vh[:, 0:n]).then_inc(sem("st_w1"), 16)
            sp.dma_start(one(w1_dram[k][1], g, cols), vl[:, 0:n]).then_inc(sem("st_w1"), 16)

        def sp_round(sp, f, last=False):
            n = NC1L if last else NC1R
            for c in range(n + 1):
                if c < n:
                    w1_load(sp, NC1R * f + c, *w1_chunk(f, c))
                if c:
                    w1_store(sp, NC1R * f + c - 1, *w1_chunk(f, c - 1))

        def load_x(sp, b):
            sp.wait_ge(sem("x1_sum"), NI * b)
            sp.sem_inc(sem("sp_seen"), 1)
            sp.dma_start(xin[:, :, :], x_rows[bass.ds(b, 1)].rearrange("o p i d -> (o p) i d")).then_inc(sem("ld_x"), 16)

        @block.sync
        def _(sp):
            sp.dma_start(xin[:, :, :], x_rows[0]).then_inc(sem("ld_x"), 16)
            for name, t in (("wqkvT", wqkv), ("woT", wo)):
                sp.dma_start(t[:, :, :], A[name].rearrange("(k p) n -> p k n", p=P)).then_inc(sem("ld_wa"), 16)
            sp.dma_start(costab[:, :, :], A["cos"].rearrange("(i p) n -> p i n", p=P)).then_inc(sem("ld_wa"), 16)
            sp.dma_start(sintab[:, :, :], A["sin"].rearrange("(i p) n -> p i n", p=P)).then_inc(sem("ld_wa"), 16)
            sp.dma_start(shift[:, :], A["shift"]).then_inc(sem("ld_shift"), 16)
            for n, k in enumerate("gud"):
                G, N8 = (KD, INTER0 // PACK) if k in "gu" else (f0.n, D // PACK)
                if n:
                    sp.wait_ge(sem("zk_done"), n)
                sp.dma_start(zk[0:G, 0:N8], A[f"z0{k}"]).then_inc(sem("ld_zk"), 16)
                sp.wait_ge(sem("zs_done"), n + 1)
                sp.dma_start(zs_dram[k][0:G, 0:N8 * PACK], zs[0:G, 0:N8 * PACK]).then_inc(sem("st_zs"), 16)
            for c, (k, g, c0, n) in enumerate(CH0):
                r = rows0(k, g)
                mi = "gud".index(k)
                sp.wait_ge(sem("st_zs"), 16 * (mi + 1))
                if c >= 2:
                    sp.wait_ge(sem("deq_d"), c - 1)
                src = bcast(A[f"q0{k}"][g * 16:g * 16 + r // PACK, c0:c0 + n], 1, PACK)
                sp.dma_start(pk[0:r, c % 2, 0:n], src).then_inc(sem(f"ld_pk{c % 2}"), 16)
                sp.dma_start(zb[0:r, c % 2, 0:n], zs_dram[k][g, c0:c0 + n].partition_broadcast(r)).then_inc(sem(f"ld_pk{c % 2}"), 16)
                sp.dma_start(w0[k][1][0:r, g, c0:c0 + n], A[f"s0{k}"][g, c0:c0 + n].partition_broadcast(r)).then_inc(sem(f"ld_pk{c % 2}"), 16)
            load_x(sp, 1)
            sp.wait_ge(sem("w0_ready"), 1)
            with sp.Fori(0, NB - 2) as f:
                sp_round(sp, f)
                load_x(sp, f + 2)
            sp_round(sp, NB - 2)
            sp_round(sp, NB - 1, last=True)
            sp.wait_ge(sem("loop_act"), 1)
            sp.wait_ge(sem("loop_dve"), 1)
            sp.wait_ge(sem("loop_pe"), 1)
            sp.wait_ge(sem("loop_pool"), 1)
            sp.wait_ge(sem("st_x2"), 16 * NT)
            sp.dma_start(x2a[:, :, :], x2_blocks[0]).then_inc(sem("ld_x2"), 16)
            sp.dma_start(wdT[:, :, :], A["wdT"].rearrange("(k p) n -> p k n", p=P)).then_inc(sem("ld_wd"), 16)
            sp.dma_start(bdn[:, :], A["bdn"].rearrange("(p o) -> p o", o=1)).then_inc(sem("ld_wd"), 16)
            ld = []
            ld.append((inwT[:, :], A["inwT"]))
            ld.append((owT[:, :, :], A["owT"].rearrange("(k p) n -> p k n", p=P)))
            ld.append((wuT[:, :], A["wuT"]))
            ld.append((bup[:, :], A["bup"].partition_broadcast(P)))
            ld.append((convw[:, :, :], A["convw"].partition_broadcast(P)))
            ld.append((convb[:, :], A["convb"].partition_broadcast(P)))
            ld.append((fcD[:, :, :], A["fcD"].partition_broadcast(P)))
            for half in range(2):
                ld.append((A8[:, half * NHY:half * NHY + NHY], A["Alog"].partition_broadcast(P)))
                ld.append((dtb8[:, half * NHY:half * NHY + NHY], A["dtb"].partition_broadcast(P)))
            ld.append((D4[:, :], A["D"].partition_broadcast(P)))
            ld.append((nw[:, :], A["nw"]))
            ld.append((al[:, 0:1], A["gate"].partition_broadcast(P)))
            assert len(ld) == NLD1
            for dst, src in ld:
                sp.dma_start(dst, src).then_inc(sem("ld_w1"), 16)
            sp.wait_ge(sem("st_w1"), 32 * NC1)
            for k in "gud":
                for part in range(2):
                    sp.dma_start(w1[k][part][:, :, :], w1_dram[k][part].rearrange("g p n -> p g n")).then_inc(sem("ld_wf"), 16)

            def results(f):
                for l in range(NB):
                    sp.wait_ge(sem("out_ready"), NB * f + l + 1)
                    sp.sem_inc(sem("sp_seen"), 1)
                    sp.dma_start(out_tiles[l, bass.ds(f, 1)].rearrange("o p d -> (o p) d"), x3r[:, l, :]).then_inc(sem("st_out"), 16)

            def load_x2(s):
                sp.wait_ge(sem("x3_sum"), NB * s)
                sp.sem_inc(sem("sp_seen"), 1)
                sp.dma_start(x2a[:, :, :], x2_blocks[bass.ds(s, 1)].rearrange("o p l d -> (o p) l d")).then_inc(sem("ld_x2"), 16)

            load_x2(1)
            with sp.Fori(0, NI - 2) as f:
                load_x2(f + 2)
                results(f)
            results(NI - 2)
            results(NI - 1)
            sp.wait_ge(sem("st_out"), 16 * NT)

        def w1_prep(pool, own, c, n):
            pool.wait_ge(sem("ld_w1c"), 48 * (c + 1))
            q, z, hi, lo = (t[:, 0:n] for t in (vq, vz, vh, vl))
            own.link(pool.tensor_tensor(q.bitcast(I32), q.bitcast(I32), z, ALU.subtract))
            pool.sem_inc(sem("w1_i"), 1)
            own.link(pool.tensor_scalar(q, q.bitcast(I32), W_SCALE, 0.0, ALU.mult, ALU.add))
            own.link(pool.tensor_tensor(q, q, vs[:, 0:n], ALU.mult))
            pool.sem_inc(sem("w1_i"), 1)
            pool.wait_ge(sem("st_w1"), 32 * c)
            pool.sem_inc(sem("w1_i"), 1)
            own.link(pool.tensor_scalar(hi, q, 1.0, 0.0, ALU.mult, ALU.add))
            pool.tensor_tensor(lo, q, hi, ALU.subtract).then_inc(sem("w1_lo"), 1)

        def round_pool(pool, own, b, f):
            if b is not None and f is not None:
                pool.wait_ge(sem("fxl"), NI * b)
                pool.sem_inc(sem("stk_free"), 1)
                pool.memset(stk[:, :, 0, 1, :, :], 0.0)
                pool.memset(stk[:, :, 1, 0, :, :], 0.0).then_inc(sem("stk_zero"), 1)
            for u in range(UEND):
                if f is None and u in CH0_AT:
                    k, g, c0, n = CH0[CH0_AT[u]]
                    r = rows0(k, g)
                    hi, lo = (w0[k][p][0:r, g, c0:c0 + n] for p in (0, 1))
                    pool.wait_ge(sem("deq_d"), CH0_AT[u] + 1)
                    own.link(pool.tensor_tensor(wv[0:r, 0:n], hi, lo, ALU.mult))
                    own.link(pool.tensor_scalar(hi, wv[0:r, 0:n], 1.0, 0.0, ALU.mult, ALU.add))
                    own.link(pool.tensor_tensor(lo, wv[0:r, 0:n], hi, ALU.subtract))
                    if CH0_AT[u] == len(CH0) - 1:
                        pool.sem_inc(sem("w0_ready"), 1)
                if f is not None and u in W1_AT and W1_AT[u] < (NC1R if b is not None else NC1L):
                    c = W1_AT[u]
                    w1_prep(pool, own, NC1R * f + c, w1_chunk(f, c)[3])
                if b is not None:
                    for i in range(NI):
                        if u == LAST[i] + 12:
                            pool.wait_ge(sem("ve1"), NI * b + i + 1)
                            pool.tensor_tensor(rstd[:, i % 2:i % 2 + 1], ve[:, i % 2:i % 2 + 1], neghalf[:, 0:1], ALU.pow).then_inc(sem("rstd1"), 1)
                if f is not None:
                    if u - 3 in U_AT:
                        n = U_AT[u - 3]
                        j, half = divmod(n, 2)
                        r, cols = f0.tiles[j][1], slice(half * H2, half * H2 + H2)
                        pool.wait_ge(sem("f0_hi"), NGU * f + n + 1)
                        pool.tensor_tensor(int0[1][0:r, j, cols], prod[0:r, n % 2, :], int0[0][0:r, j, cols], ALU.subtract).then_inc(sem("f0_lo"), 1)
                    if u - 1 in Y_AT:
                        i = Y_AT[u - 1]
                        pool.wait_ge(sem("ve2"), NI * f + i + 1)
                        pool.tensor_tensor(rstdb[:, i % 2:i % 2 + 1], veb[:, i % 2:i % 2 + 1], neghalf[:, 0:1], ALU.pow).then_inc(sem("rstd2"), 1)
                        pool.wait_ge(sem("x2_done"), NI * f + i + 1)
                        pool.dma_start(x2_dram[bass.ds(NI * f + i, 1)].rearrange("o p d -> (o p) d"), x1r[:, i, :]).then_inc(sem("st_x2"), 16)

        def round1_pool(pool, s, f):
            def ffn(u):
                if f is not None:
                    if u - 2 in GU1_AT:
                        n = GU1_AT[u - 2]
                        j, half = divmod(n, 2)
                        cols = slice(half * H2, half * H2 + H2)
                        pool.wait_ge(sem("f1_hi"), NG1 * f + n + 1)
                        pool.tensor_tensor(int1[1][:, j, cols], prod1[:, n % 2, :], int1[0][:, j, cols], ALU.subtract).then_inc(sem("f1_lo"), 1)
                    if u in OUT1_AT:
                        i = OUT1_AT[u]
                        pool.wait_ge(sem("ve4"), NB * f + i + 1)
                        pool.tensor_tensor(rstdd[:, i % 2:i % 2 + 1], ved[:, i % 2:i % 2 + 1], neghalf[:, 0:1], ALU.pow).then_inc(sem("rstd4"), 1)

            def adapter(u):
                if s is not None:
                    for p in range(2):
                        q, at = 2 * s + p, u - PASS_AT[p]
                        if at == 1:
                            pool.wait_ge(sem("h_raw"), q + 1)
                            for j in (1, 2, 3):
                                ins = pool.tensor_tensor(conv_t[j], xraw[:, 0:NB - j, :], bcast(convw[:, 3 - j, :], 1, NB - j), ALU.mult)
                            ins.then_inc(sem("h_taps"), 1)
                        if at == 9:
                            pool.wait_ge(sem("h_M"), q + 1)
                            for m, t in ((3, yp[:, :, :]), (2, yq)):
                                pool.tensor_tensor(t.rearrange("p l (h c) -> p l h c", h=NHY), xs_b(m), m_b(m), ALU.mult).then_inc(sem("h_yp"), 1)
                        if at == 12:
                            pool.wait_ge(sem("h_ss"), q + 1)
                            pool.sem_inc(sem("h_ss_seen"), 1)
                            pool.tensor_scalar(rs[:, :], ss[:, :], 1.0 / DIN, EPS, ALU.mult, ALU.add).then_inc(sem("h_ve"), 1)
                            pool.wait_ge(sem("h_ve"), q + 1)
                            pool.tensor_tensor(rs[:, :], rs[:, :], neghalf[:, :], ALU.pow).then_inc(sem("h_rs"), 1)
                    if u == MIX + 3:
                        pool.wait_ge(sem("ve3"), NB * s + NB)
                        pool.tensor_tensor(rstdc[:, :], vec[:, :], neghalf[:, :], ALU.pow).then_inc(sem("rstd3"), 1)

            for u in range(UEND1):
                if u < MIX:
                    ffn(u)
                adapter(u)
                if u >= MIX:
                    ffn(u)

        def layer1_pool(pool):
            pool.wait_ge(sem("loop_act"), 1)
            pool.wait_ge(sem("loop_dve"), 1)
            pool.wait_ge(sem("loop_pe"), 1)
            round1_pool(pool, 0, None)
            with pool.Fori(0, NI - 1) as f:
                round1_pool(pool, f + 1, f)
            round1_pool(pool, None, NI - 1)

        @block.gpsimd
        def _(pool):
            own = Own(pool, sem("own_pool"))
            own.did(pool.memset(identf[:, :], 0.0))
            own.did(pool.memset(identh[:, :], 0.0))
            own.did(pool.memset(identb[:, :], 0.0))
            own.link(pool.memset(mask[:, :], 0.0))
            for t in (identf, identh, identb):
                own.did(pool.affine_select(out=t[:, :], in_=t[:, :], compare_op=ALU.not_equal, fill=1.0, base=0,
                                           pattern=[[-1, P]], channel_multiplier=1))
            own.did(pool.affine_select(out=mask[:, :], in_=mask[:, :], compare_op=ALU.is_ge, fill=MASKED, base=0,
                                       pattern=[[-1, P]], channel_multiplier=1))
            own.did(pool.memset(neghalf[:, :], -0.5))
            own.did(pool.memset(V[:, :, :, 2 * HD + 1:VW], 0.0))
            own.did(pool.memset(stk[:, :, :, :, :, :], 0.0))
            own.link(pool.memset(V[:, :, :, 2 * HD:2 * HD + 1], 1.0))
            pool.sem_inc(sem("consts"), 1)
            round_pool(pool, own, 0, None)
            with pool.Fori(0, NB - 1) as f:
                own.enter(f, POOL_LOOP)
                round_pool(pool, own, f + 1, f)
                own.leave(NB - 1)
            round_pool(pool, own, None, NB - 1)
            pool.sem_inc(sem("loop_pool"), 1)
            layer1_pool(pool)

        def stage_act(act, b, i):
            act.wait_ge(sem("qk"), NI * b + i + 1)
            if i:
                act.wait_ge(sem("str"), 4 * NI * b + 4 * i)
            q = qk[:, i % 2, 0:NH * HD].rearrange("p (h c) -> p h c", h=NH)
            k = qk[:, i % 2, NH * HD:QK].rearrange("p (h c) -> p h c", h=NKV)
            act.activation(stq[:, :, 0:4:2, :], bcast(q, 2, 2), ACT.Copy, scale=HD ** -0.5)
            act.activation(stk[:, :, 0, 0, 0:2, :], bcast(k, 2, 2), ACT.Copy)
            act.activation(stk[:, :, 1, 1, 0:2, :], bcast(k, 2, 2), ACT.Copy)
            vp = ps[:, 1 + 2 * (i % 2), QK - 512:QKV - 512].rearrange("p (g c) -> p g c", g=NKV)
            act.activation(V[:, i, :, 0:HD], vp, ACT.Copy).then_inc(sem("st_hi"), 1)
            for gi in (0, 2):
                act.wait_ge(sem("str"), 4 * NI * b + 4 * i + gi + 1)
                dst = (qT if gi < 2 else kT)[:, 0:8, i * P:(i + 1) * P]
                act.activation(dst, ps[:, 4, :].bitcast(F16).rearrange("p (a n) -> p a n", a=8), ACT.Copy).then_inc(sem("ste_act"), 1)

        def projections_act(act, b):
            for i in range(NI):
                act.wait_ge(sem("xtr"), NI * b + i + 1)
                if i >= 2:
                    act.wait_ge(sem("proj"), NI * b + i - 1)
                act.activation(xT[:, i % 2, :, :].rearrange("p k n -> p (k n)"), ps[:, 6 + i % 2, :], ACT.Copy).then_inc(sem("xte"), 1)
                if i >= 1:
                    stage_act(act, b, i - 1)
            stage_act(act, b, NI - 1)

        def ffn0_input_act(act, b, i):
            act.wait_ge(sem("ftr"), NI * b + i + 1)
            act.activation(xh[:, :, i * P:(i + 1) * P], ps[:, 6, :].rearrange("p (k n) -> p k n", k=KD), ACT.Copy).then_inc(sem("fxh"), 1)

        def round_act(act, b, f):
            if b is not None:
                projections_act(act, b)
            for u in range(UEND):
                if f is not None and u - 1 in U_AT:
                    n = U_AT[u - 1]
                    r = f0.tiles[n // 2][1]
                    act.wait_ge(sem("f0_gu"), NGU * f + n + 1)
                    if n >= 2:
                        act.wait_ge(sem("f0_prod"), NGU * f + n - 1)
                    act.activation(sg[0:r, n % 2, :], ps[0:r, gu_bank(b, n), 0:H2], ACT.Tanh, scale=0.5 / W_SCALE).then_inc(sem("f0_sg"), 1)
                if b is not None:
                    if 2 <= u <= NU + 1:
                        v = u - 2
                        i, w, h0, g = UNITS[v]
                        act.wait_ge(sem("ptr"), NU * b + v + 1)
                        if v >= 3:
                            act.wait_ge(sem("pv"), NU * b + v - 2)
                        act.activation(pth[:, v % 3, 0:g * w], ps[:, 2 + v % 2, 0:g * w], ACT.Copy).then_inc(sem("pth"), 1)
                    if u < NU:
                        i, w, h0, g = UNITS[u]
                        act.wait_ge(sem("nmax"), NU * b + u + 1)
                        if u >= 2:
                            act.wait_ge(sem("ptr"), NU * b + u - 1)
                        for x in range(g):
                            ins = act.activation(Pe[:, u % 2, x * w:(x + 1) * w], ps[:, u % 2, x * w:(x + 1) * w], ACT.Exp,
                                                 bias=nmax[:, u % 4, x:x + 1])
                        ins.then_inc(sem("exp"), 1)
                    for i in range(NI):
                        if u == LAST[i] + 8:
                            act.wait_ge(sem("atr"), NI * b + i + 1)
                            act.activation(aT[:, :, :].rearrange("p k n -> p (k n)"), ps[:, 6, :], ACT.Copy).then_inc(sem("ate"), 1)
                    if u - 1 in FTR_AT:
                        ffn0_input_act(act, b, FTR_AT[u - 1])
                if f is not None:
                    if u - 3 in U_AT:
                        n = U_AT[u - 3]
                        j, half = divmod(n, 2)
                        r = f0.tiles[j][1]
                        act.wait_ge(sem("f0_prod"), NGU * f + n + 1)
                        act.activation(int0[0][0:r, j, half * H2:half * H2 + H2], prod[0:r, n % 2, :], ACT.Copy).then_inc(sem("f0_hi"), 1)
                    if u in Y_AT:
                        i = Y_AT[u]
                        act.wait_ge(sem("f0_down"), NI * f + i + 1)
                        if i >= 2:
                            act.wait_ge(sem("x2_sum"), NI * f + i - 1)
                        act.activation(y16[:, i % 2, :], ps[:, down_bank(b, i), :], ACT.Copy, scale=1.0 / W_SCALE).then_inc(sem("y16"), 1)
            if b is not None:
                ffn0_input_act(act, b, NI - 1)

        def ssm_input_act(act, q):
            act.wait_ge(sem("h_in"), q + 1)
            act.activation(xraw[:, :, 0:DIN], ps[:, 2:2 + NB, DIN:2 * DIN], ACT.Copy)
            bc = ps[:, 7, 0:NB * 64].rearrange("p (l c) -> p l c", l=NB)
            act.activation(xraw[:, :, DIN:CONV], bc[:, :, 0:2 * DST], ACT.Copy)
            act.activation(dtr[:, :, :], bc[:, :, 2 * DST:2 * DST + 2 * NHY], ACT.Copy).then_inc(sem("h_raw"), 1)
            act.activation(zg[:, :, :], ps[:, 2:2 + NB, 0:DIN], ACT.Silu).then_inc(sem("h_z"), 1)

        def adapter_input_act(act, s, at):
            if at == 0:
                for l in range(NB):
                    act.wait_ge(sem("c1_tr"), NB * s + l + 1)
                    act.activation(xTb[:, :, l * P:(l + 1) * P], ps[:, 2 + l, :].rearrange("p (k n) -> p k n", k=KD), ACT.Copy).then_inc(sem("c1_te"), 1)
            if at == 1:
                act.wait_ge(sem("c1_dn"), s + 1)
                act.activation(xmid[:, :], ps[:, 6, :], ACT.Gelu, bias=bdn[:, 0:1]).then_inc(sem("xmid"), 1)
            if at == 2:
                ssm_input_act(act, 2 * s)

        def round1_act(act, s, f, more):
            for u in range(UEND1):
                if f is not None:
                    if u - 1 in GU1_AT:
                        n = GU1_AT[u - 1]
                        act.wait_ge(sem("f1_gu"), NG1 * f + n + 1)
                        if n >= 2:
                            act.wait_ge(sem("f1_prod"), NG1 * f + n - 1)
                        act.activation(sg1[:, n % 2, :], ps[:, n % 2, 0:H2], ACT.Silu, scale=1.0 / W_SCALE).then_inc(sem("f1_sg"), 1)
                    if u - 2 in GU1_AT:
                        n = GU1_AT[u - 2]
                        j, half = divmod(n, 2)
                        act.wait_ge(sem("f1_prod"), NG1 * f + n + 1)
                        act.activation(int1[0][:, j, half * H2:half * H2 + H2], prod1[:, n % 2, :], ACT.Copy).then_inc(sem("f1_hi"), 1)
                if s is not None:
                    if more:
                        adapter_input_act(act, s + 1, u - HEAD)
                    for p in range(2):
                        q, at = 2 * s + p, u - PASS_AT[p]
                        if at == 0 and p:
                            ssm_input_act(act, q)
                        if at == 2:
                            act.wait_ge(sem("h_v"), q + 1)
                            act.activation(sm["e"][:, :, :], sm["e"][:, :, :], ACT.Exp, scale=-1.0).then_inc(sem("h_e"), 1)
                        if at == 3:
                            act.wait_ge(sem("h_conv"), q + 1)
                            act.activation(xc[:, :, :], yc[:, :, :], ACT.Silu).then_inc(sem("h_x"), 1)
                        if at == 4:
                            act.wait_ge(sem("h_adt"), q + 1)
                            act.activation(sm["da"][:, :, :], sm["da"][:, :, :], ACT.Exp).then_inc(sem("h_da"), 1)
                        if at == 12:
                            act.wait_ge(sem("h_y"), q + 1)
                            for l in range(NB):
                                ins = act.activation(ty[:, l, :], yy[:, l, :], ACT.Square, accum_out=ss[:, l:l + 1])
                            ins.then_inc(sem("h_ss"), 1)
                        if at == 14:
                            act.wait_ge(sem("h_ytr"), q + 1)
                            act.activation(yT[:, :, :], ps[:, 2:4, :], ACT.Copy).then_inc(sem("h_yT"), 1)
                    if u == MIX + 5:
                        for l in range(NB):
                            act.wait_ge(sem("x3tr"), NB * s + l + 1)
                            act.activation(x3h[:, :, l * P:(l + 1) * P], ps[:, 2 + l, :].rearrange("p (k n) -> p k n", k=KD), ACT.Copy).then_inc(sem("x3h"), 1)

        def layer1_act(act):
            act.wait_ge(sem("loop_dve"), 1)
            act.wait_ge(sem("loop_pe"), 1)
            act.wait_ge(sem("loop_pool"), 1)
            for at in range(3):
                if at == 1:
                    act.wait_ge(sem("ld_wd"), 32)
                if at == 2:
                    act.wait_ge(sem("alog"), 1)
                    act.activation(A8[:, :], A8[:, :], ACT.Exp)
                    act.activation(al[:, 1:2], al[:, 0:1], ACT.Exp, scale=-1.0).then_inc(sem("c_exp"), 1)
                adapter_input_act(act, 0, at)
            round1_act(act, 0, None, True)
            with act.Fori(0, NI - 2) as f:
                round1_act(act, f + 1, f, True)
            round1_act(act, NI - 1, NI - 2, False)
            round1_act(act, None, NI - 1, False)

        @block.scalar
        def _(act):
            act.wait_ge(sem("consts"), 1)
            round_act(act, 0, None)
            with act.Fori(0, NB - 1) as f:
                round_act(act, f + 1, f)
            round_act(act, None, NB - 1)
            act.sem_inc(sem("loop_act"), 1)
            layer1_act(act)

        def layer_norm_1(dve, own, r, st, m, v, ready):
            own.link(dve.bn_stats(st[:, :], r))
            dve.sem_inc(sem("bn"), 1)
            own.link(dve.bn_aggr(m, st[:, :]))
            dve.tensor_scalar(v, m[:, 1:2], EPS, None, ALU.add).then_inc(ready, 1)

        def rope(dve, own, b, i):
            dve.wait_ge(sem("proj"), NI * b + i + 1)
            base = 2 * (i % 2)
            src = ps[:, base:base + 2, :].rearrange("p k n -> p (k n)")[:, 0:QK].rearrange("p (h c t) -> p h c t", h=NH + NKV, t=2)
            cs, sn = (t[:, i, :] for t in (costab, sintab))
            d_c = qk_c[:, :].rearrange("p (h c) -> p h c", h=NH + NKV)
            d_s = qk_s[:, :].rearrange("p (h c t) -> p h c t", h=NH + NKV, t=2)
            own.did(dve.tensor_tensor(d_c, src.rearrange("p h c t -> p h (c t)"), bcast(cs, 1, NH + NKV), ALU.mult))
            s2 = sn.rearrange("p (c t) -> p c t", t=2)
            own.did(dve.tensor_tensor(d_s[:, :, :, 0], src[:, :, :, 1], bcast(s2[:, :, 0], 1, NH + NKV), ALU.mult))
            own.link(dve.tensor_tensor(d_s[:, :, :, 1], src[:, :, :, 0], bcast(s2[:, :, 1], 1, NH + NKV), ALU.mult))
            dve.tensor_tensor(qk[:, i % 2, :], qk_c[:, :], qk_s[:, :], ALU.add).then_inc(sem("qk"), 1)
            dve.wait_ge(sem("st_hi"), NI * b + i + 1)
            q = qk[:, i % 2, 0:NH * HD].rearrange("p (h c) -> p h c", h=NH)
            k = qk[:, i % 2, NH * HD:QK].rearrange("p (h c) -> p h c", h=NKV)
            for c in (0, 2):
                own.did(dve.scalar_tensor_tensor(out=stq[:, :, c + 1, :], in0=q, scalar=HD ** -0.5, in1=stq[:, :, c, :], op0=ALU.mult, op1=ALU.subtract))
            for v in (0, 1):
                own.did(dve.tensor_tensor(stk[:, :, v, v, 2:4, :], bcast(k, 2, 2), stk[:, :, v, v, 0:2, :], ALU.subtract))
            vp = ps[:, base + 1, QK - 512:QKV - 512].rearrange("p (g c) -> p g c", g=NKV)
            own.link(dve.tensor_tensor(V[:, i, :, HD:2 * HD], vp, V[:, i, :, 0:HD], ALU.subtract))
            dve.sem_inc(sem("st_lo"), 1)
            for gi in (1, 3):
                dve.wait_ge(sem("str"), 4 * NI * b + 4 * i + gi + 1)
                dst = (qT if gi < 2 else kT)[:, 8:16, i * P:(i + 1) * P]
                dve.tensor_copy(dst, ps[:, 5, :].bitcast(F16).rearrange("p (a n) -> p a n", a=8)).then_inc(sem("ste_dve"), 1)

        def out_bank(dve, own, b, v):
            n = OG_END[v]
            i, q = n // NOG, n % NOG
            dve.wait_ge(sem("pv"), NU * b + v + 1)
            if q == 0 and i >= 2:
                dve.wait_ge(sem("atr"), NI * b + i - 1)
            O = ps[:, 4 + n % 2, :].rearrange("p (h c) -> p h c", h=OG)
            own.did(dve.tensor_reduce(osum[:, :, :], O[:, :, 0:2 * HD].rearrange("p h (t c) -> p h c t", t=2), AX, ALU.add))
            own.link(dve.reciprocal(rinv[:, :], O[:, :, 2 * HD]))
            dve.sem_inc(sem("o_read"), 1)
            own.link(dve.tensor_tensor(attn[:, i % 2, q * OG * HD:(q + 1) * OG * HD].rearrange("p (h c) -> p h c", h=OG), osum[:, :, :],
                                       bcast(rinv[:, :], 2, HD), ALU.mult))
            if q == NOG - 1:
                dve.sem_inc(sem("attn"), 1)

        def ffn0_input_dve(dve, b, i):
            dve.wait_ge(sem("fxh"), NI * b + i + 1)
            dve.tensor_tensor(xl[:, :, i * P:(i + 1) * P], ps[:, 6, :].rearrange("p (k n) -> p k n", k=KD), xh[:, :, i * P:(i + 1) * P],
                              ALU.subtract).then_inc(sem("fxl"), 1)

        def dequant_dve(dve, own, c):
            k, g, c0, n = CH0[c]
            r = rows0(k, g)
            dve.wait_ge(sem(f"ld_pk{c % 2}"), 48 * (c // 2 + 1))
            own.link(dve.tensor_scalar(nib[0:r, c % 2, 0:n], pk[0:r, c % 2, 0:n], shift[0:r, 0:1], 15, ALU.logical_shift_right, ALU.bitwise_and))
            dve.scalar_tensor_tensor(out=w0[k][0][0:r, g, c0:c0 + n], in0=nib[0:r, c % 2, 0:n], scalar=W_SCALE,
                                     in1=zb[0:r, c % 2, 0:n], op0=ALU.mult, op1=ALU.subtract).then_inc(sem("deq_d"), 1)

        def round_dve(dve, own, b, f):
            if f is not None:
                dve.wait_ge(sem("w0_ready"), 1)
                own.link(dve.tensor_copy(x1r[:, :, :], x1[:, :, :]))
            if b is not None:
                for i in range(NI):
                    rope(dve, own, b, i)
            for u in range(UEND):
                if b is not None and 3 <= u <= NU + 2:
                    v = u - 3
                    i, w, h0, g = UNITS[v]
                    dve.wait_ge(sem("pth"), NU * b + v + 1)
                    if v >= 3:
                        dve.wait_ge(sem("pv"), NU * b + v - 2)
                    dve.tensor_tensor(ptl[:, v % 3, 0:g * w], ps[:, 2 + v % 2, 0:g * w], pth[:, v % 3, 0:g * w], ALU.subtract).then_inc(sem("ptl"), 1)
                if f is not None and u - 2 in U_AT:
                    n = U_AT[u - 2]
                    r = f0.tiles[n // 2][1]
                    dve.wait_ge(sem("f0_m"), NGU * f + n + 1)
                    if n >= 2:
                        dve.wait_ge(sem("f0_hi"), NGU * f + n - 1)
                        dve.wait_ge(sem("f0_lo"), NGU * f + n - 1)
                    dve.scalar_tensor_tensor(out=prod[0:r, n % 2, :], in0=ps[0:r, gu_bank(b, n), H2:S], scalar=0.5 / W_SCALE ** 2,
                                             in1=sg[0:r, n % 2, :], op0=ALU.mult, op1=ALU.mult).then_inc(sem("f0_prod"), 1)
                if b is not None and u < NU:
                    i, w, h0, g = UNITS[u]
                    dve.wait_ge(sem("score"), NU * b + u + 1)
                    if u >= 4:
                        dve.wait_ge(sem("exp"), NU * b + u - 3)
                    dve.tensor_reduce(nmax[:, u % 4, 0:g], ps[:, u % 2, 0:g * w].rearrange("p (g w) -> p g w", g=g), AX, ALU.max,
                                      negate=True).then_inc(sem("nmax"), 1)
                if f is None and u in CH0_AT:
                    dequant_dve(dve, own, CH0_AT[u])
                if f is not None and u - 1 in U_AT:
                    n = U_AT[u - 1]
                    r = f0.tiles[n // 2][1]
                    dve.wait_ge(sem("f0_sg"), NGU * f + n + 1)
                    dve.scalar_tensor_tensor(out=sg[0:r, n % 2, :], in0=sg[0:r, n % 2, :], scalar=1.0, in1=ps[0:r, gu_bank(b, n), 0:H2],
                                             op0=ALU.add, op1=ALU.mult).then_inc(sem("f0_m"), 1)
                if b is not None:
                    if u - 5 in OG_END:
                        out_bank(dve, own, b, u - 5)
                    for i in range(NI):
                        if u == LAST[i] + 11:
                            dve.wait_ge(sem("wo"), NI * b + i + 1)
                            own.link(dve.tensor_tensor(x1[:, i, :], ps[:, 6, :], xin[:, i, :], ALU.add))
                            dve.sem_inc(sem("x1_sum"), 1)
                            layer_norm_1(dve, own, x1[:, i, :], st6, mv[:, i % 2, :], ve[:, i % 2:i % 2 + 1], sem("ve1"))
                        if u == LAST[i] + 14:
                            dve.wait_ge(sem("rstd1"), NI * b + i + 1)
                            own.link(dve.tensor_scalar(x1[:, i, :], x1[:, i, :], mv[:, i % 2, 0:1], rstd[:, i % 2:i % 2 + 1], ALU.subtract, ALU.mult))
                            dve.sem_inc(sem("x1"), 1)
                    if u - 2 in FTR_AT:
                        ffn0_input_dve(dve, b, FTR_AT[u - 2])
                if f is not None:
                    if u - 1 in Y_AT:
                        i = Y_AT[u - 1]
                        dve.wait_ge(sem("y16"), NI * f + i + 1)
                        own.link(dve.tensor_tensor(x1r[:, i, :], y16[:, i % 2, :], x1r[:, i, :], ALU.add))
                        dve.sem_inc(sem("x2_sum"), 1)
                        layer_norm_1(dve, own, x1r[:, i, :], st6b, mvb[:, i % 2, :], veb[:, i % 2:i % 2 + 1], sem("ve2"))
                    if u - 3 in Y_AT:
                        i = Y_AT[u - 3]
                        dve.wait_ge(sem("rstd2"), NI * f + i + 1)
                        dve.tensor_scalar(x1r[:, i, :], x1r[:, i, :], mvb[:, i % 2, 0:1], rstdb[:, i % 2:i % 2 + 1], ALU.subtract,
                                          ALU.mult).then_inc(sem("x2_done"), 1)
            if b is not None:
                ffn0_input_dve(dve, b, NI - 1)
                if f is not None:
                    dve.wait_ge(sem("st_x2"), 16 * NI * (f + 1))

        def hydra_dve(dve, own, s, p, at):
            q = 2 * s + p
            fl = lambda a: a.rearrange("p a b -> p (a b)")
            v, e, mx, w, w2, po, dt, da = (sm[n][:, :, :] for n in ("v", "e", "mx", "w", "w2", "p", "dt", "da"))
            y4, t4 = (t[:, :, :].rearrange("p l (h c) -> p l h c", h=NHY) for t in (yy, ty))
            if at == 1:
                dve.wait_ge(sem("h_raw"), q + 1)
                own.link(dve.tensor_tensor(v, dtr[:, :, :], bcast(dtb8[:, :], 1, NB), ALU.add))
                own.did(dve.tensor_scalar(mx, v, 0.0, None, ALU.max))
                own.link(dve.scalar_tensor_tensor(out=fl(e), in0=fl(v), scalar=-1.0, in1=fl(v), op0=ALU.mult, op1=ALU.max))
                dve.sem_inc(sem("h_v"), 1)
                own.link(dve.tensor_tensor(yc[:, :, :], xraw[:, :, :], bcast(convw[:, 3, :], 1, NB), ALU.mult))
                own.link(dve.tensor_tensor(yc[:, :, :], yc[:, :, :], bcast(convb[:, :], 1, NB), ALU.add))
            if at == 3:
                dve.wait_ge(sem("h_taps"), q + 1)
                for j in (1, 2, 3):
                    own.link(dve.tensor_tensor(yc[:, j:NB, :], yc[:, j:NB, :], conv_t[j], ALU.add))
                dve.sem_inc(sem("h_conv"), 1)
            if at == 4:
                dve.wait_ge(sem("h_e"), q + 1)
                own.link(dve.tensor_scalar(w, e, 2.0, None, ALU.add))
                own.link(dve.reciprocal(w, w))
                own.link(dve.tensor_tensor(w, w, e, ALU.mult))
                own.link(dve.tensor_tensor(w2, w, w, ALU.mult))
                own.link(dve.tensor_scalar(po, w2, 1.0 / 17, None, ALU.mult))
                for odd in (15, 13, 11, 9, 7, 5, 3):
                    own.link(dve.scalar_tensor_tensor(out=fl(po), in0=fl(po), scalar=1.0 / odd, in1=fl(w2), op0=ALU.add, op1=ALU.mult))
                own.link(dve.scalar_tensor_tensor(out=fl(po), in0=fl(po), scalar=1.0, in1=fl(w), op0=ALU.add, op1=ALU.mult))
                own.link(dve.scalar_tensor_tensor(out=fl(dt), in0=fl(po), scalar=2.0, in1=fl(mx), op0=ALU.mult, op1=ALU.add))
                own.link(dve.tensor_tensor(da, dt, bcast(A8[:, :], 1, NB), ALU.mult))
                dve.sem_inc(sem("h_adt"), 1)
            if at == 5:
                dve.wait_ge(sem("h_x"), q + 1)
                prod_cb = ty[:, 0, :].rearrange("p (l m n) -> p l m n", l=NB, m=NB)
                own.link(dve.tensor_tensor(prod_cb, bcast(xc[:, :, DIN + DST:CONV], 2, NB), bcast(xc[:, :, DIN:DIN + DST], 1, NB), ALU.mult))
                own.link(dve.tensor_reduce(CB[:, :], ty[:, 0, :].rearrange("p (a n) -> p a n", n=DST), AX, ALU.add))
                for m in range(3):
                    own.did(dve.tensor_copy(Rf[:, m, m, :], dt[:, m, 0:NHY]))
                    k = own.did(dve.tensor_copy(Sb[:, m, m, :], dt[:, m + 1, NHY:2 * NHY]))
                own.wait(k)
                dve.wait_ge(sem("h_da"), q + 1)
                own.did(dve.tensor_tensor(Rf[:, 1, 0:1, :], Rf[:, 0, 0:1, :], bcast(da[:, 1, 0:NHY], 1, 1), ALU.mult))
                own.link(dve.tensor_tensor(Sb[:, 1, 2:3, :], Sb[:, 2, 2:3, :], bcast(da[:, 2, NHY:2 * NHY], 1, 1), ALU.mult))
                own.did(dve.tensor_tensor(Rf[:, 2, 0:2, :], Rf[:, 1, 0:2, :], bcast(da[:, 2, 0:NHY], 1, 2), ALU.mult))
                own.link(dve.tensor_tensor(Sb[:, 0, 1:3, :], Sb[:, 1, 1:3, :], bcast(da[:, 1, NHY:2 * NHY], 1, 2), ALU.mult))
                for l in range(3):
                    own.did(dve.tensor_tensor(M[:, l + 1, 0:l + 1, :], Rf[:, l, 0:l + 1, :], bcast(CB[:, 4 * (l + 1) - 4:4 * (l + 1) - 4 + l + 1], 2, NHY), ALU.mult))
                    k = own.did(dve.tensor_tensor(M[:, l, l + 1:4, :], Sb[:, l, l:3, :],
                                                  bcast(CB[:, 4 * (l + 1) + l + 1:4 * (l + 1) + 4], 2, NHY), ALU.mult))
                own.wait(k)
            if at in (7, 8):
                marks = []
                for l in (0, 1) if at == 7 else (2, 3):
                    for h in range(NHY):
                        if len(marks) >= 3:
                            own.wait(marks[-3])
                        marks.append(own.did(dve.tensor_tensor_reduce(junk[:, len(marks) % 3, :], xc[:, l, 0:DIN], fcD[:, h, :], 1.0, 0.0,
                                                                      ALU.mult, ALU.add, Fd[:, l, h:h + 1])))
                own.wait(marks[-1])
            if at == 8:
                for l in range(NB):
                    k = own.did(dve.tensor_tensor(M[:, l, l, :], Fd[:, l, :], D4[:, :], ALU.add))
                own.wait(k)
                dve.sem_inc(sem("h_M"), 1)
            if at == 9:
                own.link(dve.tensor_tensor(y4, xs_b(0), m_b(0), ALU.mult))
                own.link(dve.tensor_tensor(t4, xs_b(1), m_b(1), ALU.mult))
                own.link(dve.tensor_tensor(y4, y4, t4, ALU.add))
            if at == 11:
                dve.wait_ge(sem("h_yp"), 2 * q + 1)
                own.link(dve.tensor_tensor(yy[:, :, :], yy[:, :, :], yp[:, :, :], ALU.add))
                dve.wait_ge(sem("h_yp"), 2 * q + 2)
                own.link(dve.tensor_tensor(yy[:, :, :], yy[:, :, :], yq, ALU.add))
                dve.wait_ge(sem("h_z"), q + 1)
                own.link(dve.tensor_tensor(yy[:, :, :], yy[:, :, :], zg[:, :, :], ALU.mult))
                dve.sem_inc(sem("h_y"), 1)
            if at == 13:
                dve.wait_ge(sem("h_rs"), q + 1)
                for l in range(NB):
                    k = own.did(dve.tensor_scalar(yy[:, l, :], yy[:, l, :], rs[:, l:l + 1], None, ALU.mult))
                own.wait(k)
                dve.sem_inc(sem("h_yn"), 1)
            if at == 15:
                dve.wait_ge(sem("h_out"), q + 1)
                own.link(dve.tensor_copy(uT[:, :], ps[:, 4, :]))
                dve.sem_inc(sem("h_done"), 1)

        def round1_dve(dve, own, s, f):
            if f is not None:
                own.link(dve.tensor_copy(x3r[:, :, :], x3[:, :, :]))
            def ffn(u):
                if f is not None:
                    if u - 1 in GU1_AT:
                        n = GU1_AT[u - 1]
                        dve.wait_ge(sem("f1_sg"), NG1 * f + n + 1)
                        if n >= 2:
                            dve.wait_ge(sem("f1_hi"), NG1 * f + n - 1)
                            dve.wait_ge(sem("f1_lo"), NG1 * f + n - 1)
                        dve.scalar_tensor_tensor(out=prod1[:, n % 2, :], in0=ps[:, n % 2, H2:S], scalar=1.0 / W_SCALE, in1=sg1[:, n % 2, :],
                                                 op0=ALU.mult, op1=ALU.mult).then_inc(sem("f1_prod"), 1)
                    if u in OUT1_AT:
                        i = OUT1_AT[u]
                        dve.wait_ge(sem("f1_down"), NB * f + i + 1)
                        own.link(dve.scalar_tensor_tensor(out=x3r[:, i, :], in0=ps[:, i % 2, :], scalar=1.0 / W_SCALE, in1=x3r[:, i, :],
                                                          op0=ALU.mult, op1=ALU.add))
                        dve.sem_inc(sem("ob_sum"), 1)
                        layer_norm_1(dve, own, x3r[:, i, :], st6d, mvd[:, i % 2, :], ved[:, i % 2:i % 2 + 1], sem("ve4"))
                    if u - 2 in OUT1_AT:
                        i = OUT1_AT[u - 2]
                        dve.wait_ge(sem("rstd4"), NB * f + i + 1)
                        own.link(dve.tensor_scalar(x3r[:, i, :], x3r[:, i, :], mvd[:, i % 2, 0:1], rstdd[:, i % 2:i % 2 + 1], ALU.subtract, ALU.mult))
                        dve.sem_inc(sem("out_ready"), 1)

            def adapter(u):
                if s is not None:
                    for p in range(2):
                        hydra_dve(dve, own, s, p, u - PASS_AT[p])
                    if u == MIX:
                        own.link(dve.tensor_scalar(uT[:, :], uT[:, :], al[:, 2:3], None, ALU.mult))
                        own.link(dve.scalar_tensor_tensor(out=uT[:, :], in0=xmid[:, :], scalar=al[:, 3:4], in1=uT[:, :], op0=ALU.mult, op1=ALU.add))
                        dve.sem_inc(sem("hT"), 1)
                    for l in range(NB):
                        if u == MIX + 1 + (l + 1) // 2:
                            dve.wait_ge(sem("up"), NB * s + l + 1)
                            own.link(dve.scalar_tensor_tensor(out=x3[:, l, :], in0=x2a[:, l, :], scalar=2.0, in1=ps[:, 2 + l, :], op0=ALU.mult, op1=ALU.add))
                            dve.sem_inc(sem("x3_sum"), 1)
                            own.link(dve.tensor_tensor(x3[:, l, :], x3[:, l, :], bup[:, :], ALU.add))
                            layer_norm_1(dve, own, x3[:, l, :], st6c, mvc[:, l, :], vec[:, l:l + 1], sem("ve3"))
                        if u == MIX + 4:
                            dve.wait_ge(sem("rstd3"), s + 1)
                            own.link(dve.tensor_scalar(x3[:, l, :], x3[:, l, :], mvc[:, l, 0:1], rstdc[:, l:l + 1], ALU.subtract, ALU.mult))
                            dve.sem_inc(sem("x3"), 1)
                        if u == MIX + 5:
                            dve.wait_ge(sem("x3h"), NB * s + l + 1)
                            dve.tensor_tensor(x3l[:, :, l * P:(l + 1) * P], ps[:, 2 + l, :].rearrange("p (k n) -> p k n", k=KD),
                                              x3h[:, :, l * P:(l + 1) * P], ALU.subtract).then_inc(sem("x3l"), 1)

            for u in range(UEND1):
                if u < MIX:
                    ffn(u)
                adapter(u)
                if u >= MIX:
                    ffn(u)
            if f is not None:
                dve.wait_ge(sem("st_out"), 16 * NB * (f + 1))

        def layer1_dve(dve, own):
            dve.wait_ge(sem("loop_act"), 1)
            dve.wait_ge(sem("loop_pe"), 1)
            dve.wait_ge(sem("loop_pool"), 1)
            dve.wait_ge(sem("ld_w1"), 16 * NLD1)
            own.link(dve.tensor_scalar(A8[:, :], A8[:, :], 80.0, None, ALU.min))
            dve.sem_inc(sem("alog"), 1)
            for k in range(2):
                own.did(dve.tensor_scalar(owT[:, k, :], owT[:, k, :], nw[:, k:k + 1], None, ALU.mult))
            dve.wait_ge(sem("c_exp"), 1)
            own.link(dve.tensor_scalar(al[:, 1:2], al[:, 1:2], 1.0, None, ALU.add))
            own.link(dve.reciprocal(al[:, 0:1], al[:, 1:2]))
            own.did(dve.tensor_scalar(al[:, 2:3], al[:, 0:1], -1.0, 1.0, ALU.mult, ALU.add))
            own.did(dve.tensor_scalar(al[:, 3:4], al[:, 0:1], 1.0, None, ALU.add))
            own.link(dve.tensor_scalar(A8[:, :], A8[:, :], -1.0, None, ALU.mult))
            dve.sem_inc(sem("c_small"), 1)
            round1_dve(dve, own, 0, None)
            with dve.Fori(0, NI - 1) as f:
                own.enter(f, DVE_LOOP1)
                round1_dve(dve, own, f + 1, f)
                own.leave(NI - 1)
            round1_dve(dve, own, None, NI - 1)

        @block.vector
        def _(dve):
            own = Own(dve, sem("own_dve"))
            for n, k in enumerate("gud"):
                G, N8 = (KD, INTER0 // PACK) if k in "gu" else (f0.n, D // PACK)
                dve.wait_ge(sem("ld_zk"), 16 * (n + 1))
                z8 = zi[0:G, 0:N8 * PACK].rearrange("g (n j) -> g n j", j=PACK)
                for j in range(PACK):
                    m = own.did(dve.tensor_scalar(z8[:, :, j], zk[0:G, 0:N8], 4 * j, 15, ALU.logical_shift_right, ALU.bitwise_and))
                own.wait(m)
                dve.sem_inc(sem("zk_done"), 1)
                if n:
                    dve.wait_ge(sem("st_zs"), 16 * n)
                dve.tensor_scalar(zs[0:G, 0:N8 * PACK], zi[0:G, 0:N8 * PACK], W_SCALE, W_SCALE, ALU.mult, ALU.add).then_inc(sem("zs_done"), 1)
                dve.wait_ge(sem("zs_done"), n + 1)
            dve.wait_ge(sem("ld_shift"), 16)
            dve.wait_ge(sem("ld_wa"), 64)
            dve.wait_ge(sem("consts"), 1)
            round_dve(dve, own, 0, None)
            with dve.Fori(0, NB - 1) as f:
                own.enter(f, DVE_LOOP)
                round_dve(dve, own, f + 1, f)
                own.leave(NB - 1)
            round_dve(dve, own, None, NB - 1)
            dve.sem_inc(sem("loop_dve"), 1)
            layer1_dve(dve, own)

        def stage_transposes(pe, b, i):
            pe.wait_ge(sem("st_lo"), NI * b + i + 1)
            for gi in range(4):
                n = 4 * i + gi
                if gi % 2 == 0 and n >= 2:
                    pe.wait_ge(sem("ste_act"), 2 * NI * b + n // 2)
                if gi % 2 == 1 and n >= 2:
                    pe.wait_ge(sem("ste_dve"), 2 * NI * b + n // 2)
                dst = ps[:, 4 + gi % 2, :].bitcast(F16)
                for a in range(8):
                    if gi < 2:
                        src = stq[:, 2 * (8 * gi + a):2 * (8 * gi + a) + 2, :, :].rearrange("p h c d -> p (h c d)")
                    else:
                        g, var = divmod(8 * (gi - 2) + a, 2)
                        src = stk[:, g, var, :, :, :].rearrange("p e c d -> p (e c d)")
                    ins = pe.transpose(dst[:, a * P:(a + 1) * P], src, identh[:, :])
                ins.then_inc(sem("str"), 1)

        def projections_pe(pe, b, f):
            pe.wait_ge(sem("ld_x"), 16 * (b + 1))

            def xtr(i):
                for k in range(KD):
                    ins = pe.transpose(ps[:, 6 + i % 2, k * P:(k + 1) * P], xin[:, i, k * P:(k + 1) * P], identf[:, :])
                ins.then_inc(sem("xtr"), 1)

            if f is not None:
                pe.wait_ge(sem("fxl"), NI * b)
            xtr(0)
            xtr(1)
            for i in range(NI):
                pe.wait_ge(sem("xte"), NI * b + i + 1)
                if i >= 2:
                    pe.wait_ge(sem("st_lo"), NI * b + i - 1)
                for k in range(KD):
                    pe.matmul(ps[:, 2 * (i % 2), :], xT[:, i % 2, k, :], wqkv[:, k, 0:512], start=(k == 0), stop=(k == KD - 1))
                for k in range(KD):
                    ins = pe.matmul(ps[:, 2 * (i % 2) + 1, 0:QKV - 512], xT[:, i % 2, k, :], wqkv[:, k, 512:QKV], start=(k == 0), stop=(k == KD - 1))
                ins.then_inc(sem("proj"), 1)
                if i + 2 < NI:
                    xtr(i + 2)
                if i >= 1:
                    stage_transposes(pe, b, i - 1)
            stage_transposes(pe, b, NI - 1)
            pe.wait_ge(sem("ste_act"), 2 * NI * (b + 1))
            pe.wait_ge(sem("ste_dve"), 2 * NI * (b + 1))

        def ffn0_input_pe(pe, b, i):
            pe.wait_ge(sem("x1"), NI * b + i + 1)
            pe.wait_ge(sem("x1_sum"), NI * b + max(i, NI - 2) + 1)
            if i:
                pe.wait_ge(sem("fxl"), NI * b + i)
            for k in range(KD):
                ins = pe.transpose(ps[:, 6, k * P:(k + 1) * P], x1[:, i, k * P:(k + 1) * P], identf[:, :])
            ins.then_inc(sem("ftr"), 1)

        def ffn0_gate_up_pe(pe, b, f, n, m):
            j, half = divmod(n, 2)
            c0, r = f0.tiles[j]
            cols = slice(0, H2) if m == "g" else slice(H2, S)
            if m == "g":
                before = GU_PREV[n] if b is not None else (n - 2 if n >= 2 else None)
                if before is not None:
                    pe.wait_ge(sem("f0_prod"), NGU * f + before + 1)
                if b is not None and GU_BANK[n] == 6:
                    done = sum(hi < G_SLOT[n] for lo, hi in OUT6)
                    if done:
                        pe.wait_ge(sem("x1_sum"), NI * b + done)
            at = 0
            for k in range(KD):
                for pw, px in ((0, xh), (0, xl), (1, xh)):
                    ins = pe.matmul(ps[0:r, gu_bank(b, n), cols], w0[m][pw][:, k, c0:c0 + r], px[:, k, half * H2:half * H2 + H2],
                                    start=(at == 0), stop=(at == 3 * KD - 1))
                    at += 1
            if m == "u":
                ins.then_inc(sem("f0_gu"), 1)

        def ffn0_down_pe(pe, b, f, i, piece):
            ahead = 1 if b is not None else 2
            if piece == 0:
                if i == 0:
                    pe.wait_ge(sem("f0_lo"), NGU * (f + 1))
                    pe.wait_ge(sem("f0_prod"), NGU * (f + 1))
                if i >= ahead:
                    pe.wait_ge(sem("y16"), NI * f + i - ahead + 1)
            steps = [(j, r, pi, pw) for j, (_, r) in enumerate(f0.tiles) for pi, pw in ((0, 0), (0, 1), (1, 0))]
            each = -(-len(steps) // DP)
            for at in range(piece * each, min(len(steps), piece * each + each)):
                j, r, pi, pw = steps[at]
                ins = pe.matmul(ps[:, down_bank(b, i), :], int0[pi][0:r, j, i * P:(i + 1) * P], w0["d"][pw][0:r, j, :],
                                start=(at == 0), stop=(at == len(steps) - 1))
            if piece == DP - 1:
                ins.then_inc(sem("f0_down"), 1)

        def round_pe(pe, b, f):
            if b is not None:
                if f is not None:
                    pe.wait_ge(sem("stk_zero"), f + 1)
                projections_pe(pe, b, f)
            else:
                pe.wait_ge(sem("fxl"), NI * NB)
            for u in range(UEND):
                if b is not None:
                    if u < NU:
                        i, w, h0, g = UNITS[u]
                        if u >= 2:
                            pe.wait_ge(sem("exp"), NU * b + u - 1)
                        for x in range(g):
                            h = h0 + x
                            pe.matmul(ps[:, u % 2, x * w:(x + 1) * w], qT[:, h // 2, i * P:(i + 1) * P], kT[:, 2 * (h // NREP) + h % 2, 0:w],
                                      start=True, stop=False)
                            ins = pe.matmul(ps[:, u % 2, (x + 1) * w - P:(x + 1) * w], identb[:, :], mask[:, :], start=False, stop=True)
                        ins.then_inc(sem("score"), 1)
                    if 2 <= u <= NU + 1:
                        v = u - 2
                        i, w, h0, g = UNITS[v]
                        pe.wait_ge(sem("exp"), NU * b + v + 1)
                        if v >= 2:
                            pe.wait_ge(sem("ptl"), NU * b + v - 1)
                        for c in range(0, g * w, P):
                            ins = pe.transpose(ps[:, 2 + v % 2, c:c + P], Pe[:, v % 2, c:c + P], identf[:, :])
                        ins.then_inc(sem("ptr"), 1)
                    if 4 <= u <= NU + 3:
                        v = u - 4
                        i, w, h0, g = UNITS[v]
                        pe.wait_ge(sem("ptl"), NU * b + v + 1)
                        n = i * NOG + h0 // OG
                        if h0 % OG == 0 and n >= 2:
                            pe.wait_ge(sem("o_read"), NI * NOG * b + n - 1)
                        for x in range(g):
                            h = h0 + x
                            dst = ps[:, 4 + n % 2, (h % OG) * 64:(h % OG) * 64 + VW]
                            for part, src in ((0, pth), (1, ptl)):
                                for j in range(i + 1):
                                    c = x * w + j * P
                                    ins = pe.matmul(dst, src[:, v % 3, c:c + P], V[:, j, h // NREP, :],
                                                    start=(part == 0 and j == 0), stop=(part == 1 and j == i))
                        ins.then_inc(sem("pv"), 1)
                    for i in range(NI):
                        if u == LAST[i] + 7:
                            pe.wait_ge(sem("attn"), NI * b + i + 1)
                            if f is not None:
                                pe.wait_ge(sem("f0_prod"), NGU * f + 1 + max(n for n in range(NGU) if GU_BANK[n] == 6 and G_SLOT[n] < u))
                            if i == NI - 1:
                                pe.wait_ge(sem("fxl"), NI * b + i)
                            elif i:
                                pe.wait_ge(sem("x1_sum"), NI * b + i)
                            for k in range(KD):
                                ins = pe.transpose(ps[:, 6, k * P:(k + 1) * P], attn[:, i % 2, k * P:(k + 1) * P], identf[:, :])
                            ins.then_inc(sem("atr"), 1)
                        if u == LAST[i] + 9:
                            pe.wait_ge(sem("ate"), NI * b + i + 1)
                            for k in range(KD):
                                ins = pe.matmul(ps[:, 6, :], aT[:, k, :], wo[:, k, :], start=(k == 0), stop=(k == KD - 1))
                            ins.then_inc(sem("wo"), 1)
                    if u in FTR_AT:
                        ffn0_input_pe(pe, b, FTR_AT[u])
                if f is not None:
                    if u in G_AT:
                        ffn0_gate_up_pe(pe, b, f, G_AT[u], "g")
                    if u in U_AT:
                        ffn0_gate_up_pe(pe, b, f, U_AT[u], "u")
                    if u in DOWN_AT:
                        ffn0_down_pe(pe, b, f, *DOWN_AT[u])
            if b is not None:
                ffn0_input_pe(pe, b, NI - 1)

        def ssm_input_pe(pe, u_):
            for l in range(NB):
                lhs = u_[:, l * P:(l + 1) * P]
                pe.matmul(ps[:, 2 + l, :], lhs, inwT[:, 0:512], start=True, stop=True)
                ins = pe.matmul(ps[:, 7, l * 64:l * 64 + PROJ - 512], lhs, inwT[:, 512:PROJ], start=True, stop=True)
            ins.then_inc(sem("h_in"), 1)

        def adapter_input_pe(pe, s, at, first):
            if at == 0:
                pe.wait_ge(sem("ld_x2"), 16 * (s + 1))
                if not first:
                    pe.wait_ge(sem("x3l"), NB * s)
                for l in range(NB):
                    for k in range(KD):
                        ins = pe.transpose(ps[:, 2 + l, k * P:(k + 1) * P], x2a[:, l, k * P:(k + 1) * P], identf[:, :])
                    ins.then_inc(sem("c1_tr"), 1)
            if at == 1:
                pe.wait_ge(sem("c1_te"), NB * (s + 1))
                for k in range(KD):
                    ins = pe.matmul(ps[:, 6, :], wdT[:, k, :], xTb[:, k, :], start=(k == 0), stop=(k == KD - 1))
                ins.then_inc(sem("c1_dn"), 1)
            if at == 2:
                pe.wait_ge(sem("xmid"), s + 1)
                ssm_input_pe(pe, xmid)

        def round1_pe(pe, s, f, more):
            if f is not None:
                pe.wait_ge(sem("x3l"), NB * (f + 1))
            steps = [(j, pi, pw) for j in range(f1.n) for pi, pw in ((0, 0), (0, 1), (1, 0))]
            for u in range(UEND1):
                if s is not None:
                    if more:
                        adapter_input_pe(pe, s + 1, u - HEAD, False)
                    for p in range(2):
                        q, at = 2 * s + p, u - PASS_AT[p]
                        if at == 0 and p:
                            pe.wait_ge(sem("h_done"), q)
                            ssm_input_pe(pe, uT)
                        if at == 14:
                            pe.wait_ge(sem("h_yn"), q + 1)
                            for k in range(2):
                                for l in range(NB):
                                    ins = pe.transpose(ps[:, 2 + k, l * P:(l + 1) * P], yy[:, l, k * P:(k + 1) * P], identf[:, :])
                            ins.then_inc(sem("h_ytr"), 1)
                        if at == 15:
                            pe.wait_ge(sem("h_yT"), q + 1)
                            for k in range(2):
                                ins = pe.matmul(ps[:, 4, :], owT[:, k, :], yT[:, k, :], start=(k == 0), stop=(k == 1))
                            ins.then_inc(sem("h_out"), 1)
                    if u == MIX + 1:
                        pe.wait_ge(sem("hT"), s + 1)
                        for l in range(NB):
                            pe.matmul(ps[:, 2 + l, :], uT[:, l * P:(l + 1) * P], wuT[:, :], start=True, stop=True).then_inc(sem("up"), 1)
                    if u == MIX + 5:
                        for l in range(NB):
                            pe.wait_ge(sem("x3"), NB * s + l + 1)
                            for k in range(KD):
                                ins = pe.transpose(ps[:, 2 + l, k * P:(k + 1) * P], x3[:, l, k * P:(k + 1) * P], identf[:, :])
                            ins.then_inc(sem("x3tr"), 1)
                if f is not None:
                    if u in GU1_AT:
                        n = GU1_AT[u]
                        j, half = divmod(n, 2)
                        if n >= 2:
                            pe.wait_ge(sem("f1_prod"), NG1 * f + n - 1)
                        for at_m, m in enumerate("gu"):
                            at = 0
                            for k in range(KD):
                                for pw, px in ((0, x3h), (0, x3l), (1, x3h)):
                                    ins = pe.matmul(ps[:, n % 2, at_m * H2:at_m * H2 + H2], w1[m][pw][:, k, j * P:(j + 1) * P],
                                                    px[:, k, half * H2:half * H2 + H2], start=(at == 0), stop=(at == 3 * KD - 1))
                                    at += 1
                        ins.then_inc(sem("f1_gu"), 1)
                    if u in DOWN1_AT:
                        i, piece = DOWN1_AT[u]
                        if piece == 0:
                            if i < 2:
                                pe.wait_ge(sem("f1_lo"), NG1 * (f + 1))
                            else:
                                pe.wait_ge(sem("ob_sum"), NB * f + i - 1)
                        each = len(steps) // DP1
                        for at in range(piece * each, piece * each + each):
                            j, pi, pw = steps[at]
                            ins = pe.matmul(ps[:, i % 2, :], int1[pi][:, j, i * P:(i + 1) * P], w1["d"][pw][:, j, :],
                                            start=(at == 0), stop=(at == len(steps) - 1))
                        if piece == DP1 - 1:
                            ins.then_inc(sem("f1_down"), 1)
            if f is not None:
                pe.wait_ge(sem("ob_sum"), NB * (f + 1))

        def layer1_pe(pe):
            pe.wait_ge(sem("loop_act"), 1)
            pe.wait_ge(sem("loop_dve"), 1)
            for at in range(3):
                if at == 1:
                    pe.wait_ge(sem("ld_wd"), 32)
                if at == 2:
                    pe.wait_ge(sem("ld_w1"), 16 * NLD1)
                    pe.wait_ge(sem("c_small"), 1)
                adapter_input_pe(pe, 0, at, True)
            round1_pe(pe, 0, None, True)
            pe.wait_ge(sem("ld_wf"), 16 * 6)
            with pe.Fori(0, NI - 2) as f:
                round1_pe(pe, f + 1, f, True)
            round1_pe(pe, NI - 1, NI - 2, False)
            round1_pe(pe, None, NI - 1, False)

        @block.tensor
        def _(pe):
            pe.wait_ge(sem("consts"), 1)
            pe.wait_ge(sem("ld_wa"), 64)
            round_pe(pe, 0, None)
            pe.wait_ge(sem("w0_ready"), 1)
            with pe.Fori(0, NB - 1) as f:
                round_pe(pe, f + 1, f)
            round_pe(pe, None, NB - 1)
            pe.sem_inc(sem("loop_pe"), 1)
            layer1_pe(pe)


def rope_tables():
    inv = (1.0 / 10000.0 ** (np.arange(0, HD, 2, dtype=np.float32) / HD)).astype(np.float32)
    f = np.arange(S, dtype=np.float32)[:, None] * inv[None, :]
    c, s = np.cos(f), np.sin(f)
    return np.repeat(c, 2, axis=1), np.stack([-s, s], axis=-1).reshape(S, HD)


def kernel(**inputs):
    import concourse.bacc as _bacc
    from concourse.bass_utils import run_bass_kernel_spmd as _run

    a = {k: np.asarray(v) for k, v in inputs.items()}
    cos, sin = rope_tables()
    data = {
        "x": a["L0_attn_hidden_states"],
        "wqkvT": np.concatenate([a["L0_attn_Wq"].T, a["L0_attn_Wk"].T, a["L0_attn_Wv"].T], axis=1),
        "woT": a["L0_attn_Wo"].T,
        "cos": cos, "sin": sin,
        "shift": (np.arange(P, dtype=np.int32) % PACK * 4).reshape(P, 1),
        "inwT": a["L1_attn_hy_in_w"].T, "owT": a["L1_attn_hy_out_w"].T, "wdT": a["L1_attn_w_down"].T, "wuT": a["L1_attn_w_up"].T,
        "bup": a["L1_attn_b_up"], "bdn": a["L1_attn_b_down"],
        "convw": a["L1_attn_hy_conv_w"][:, 0, -NB:].T, "convb": a["L1_attn_hy_conv_b"],
        "fcD": a["L1_attn_hy_fcD_w"], "Alog": a["L1_attn_hy_A_log"], "dtb": a["L1_attn_hy_dt_bias"], "D": a["L1_attn_hy_D"],
        "nw": a["L1_attn_hy_norm_w"].reshape(2, P).T, "gate": a["L1_attn_gate1"].reshape(1),
    }
    for k, name in (("g", "gate"), ("u", "up"), ("d", "down")):
        data[f"q0{k}"] = a[f"L0_ffn_{name}_qweight"]
        data[f"s0{k}"] = a[f"L0_ffn_{name}_scales"]
        data[f"z0{k}"] = a[f"L0_ffn_{name}_zeros"]
        data[f"q1{k}"] = a[f"L1_ffn_{name}_w"]
        data[f"s1{k}"] = a[f"L1_ffn_{name}_s"]
        data[f"z1{k}"] = a[f"L1_ffn_{name}_z"]
    data = {f"in_{k}": np.ascontiguousarray(v) for k, v in data.items()}
    nc = _bacc.Bacc("TRN2", target_bir_lowering=False, num_devices=1)
    A = {k[3:]: nc.dram_tensor(k, v.shape, mybir.dt.from_np(v.dtype), kind="ExternalInput").ap() for k, v in data.items()}
    A["out"] = nc.dram_tensor("out", (NB, S, D), F32, kind="ExternalOutput").ap()
    build(nc, A)
    return _run(nc, [data], core_ids=[0]).results[0]["out"]
```
